# Optimizing a Trainium2 kernel written in Bass

```python
import numpy as np
import jax
import jax.numpy as jnp

def _softmax(x, axis=-1):
    return jax.nn.softmax(x, axis=axis)

def _gelu(x):
    return jax.nn.gelu(x, approximate=True)

def _silu(x):
    return jax.nn.silu(x)

def _sigmoid(x):
    return jax.nn.sigmoid(x)

def _layernorm(x, axis=-1, eps=1e-05):
    m = jnp.mean(x, axis=axis, keepdims=True)
    v = jnp.var(x, axis=axis, keepdims=True)
    return (x - m) / jnp.sqrt(v + eps)

def _scatter_add(tgt, idx, src, axis=0):
    return tgt.at[idx].add(src)

def _segment_sum(src, seg, n):
    return jax.ops.segment_sum(src, seg, n)
kernel_name = 'mk_adaln_d1_jaxref_r8_98fe88'

def setup_inputs(seed: int=0):
    np.random.seed(seed)
    _w = jnp.asarray

    def _L0_attn_setup():
        import jax, jax.numpy as jnp
        import numpy as np
        EMBED_DIM = 256
        NUM_HEADS = 16
        NUM_KV_HEADS = 4
        HEAD_DIM = EMBED_DIM // NUM_HEADS
        KV_DIM = NUM_KV_HEADS * HEAD_DIM
        B, N = (2, 256)
        RMS_EPS = float(jnp.finfo(jnp.float32).eps)
        L2_EPS = 1e-12

        def _rms_norm(t):
            ms = jnp.mean(t * t, axis=-1, keepdims=True)
            return t * jax.lax.rsqrt(ms + RMS_EPS)
        key = jax.random.key(seed)
        ks = jax.random.split(key, 5)
        s = EMBED_DIM ** (-0.5)
        return {'x': jax.random.normal(ks[0], (B, N, EMBED_DIM), dtype=jnp.float32), 'Wq': jax.random.normal(ks[1], (EMBED_DIM, EMBED_DIM), dtype=jnp.float32) * s, 'Wk': jax.random.normal(ks[2], (KV_DIM, EMBED_DIM), dtype=jnp.float32) * s, 'Wv': jax.random.normal(ks[3], (KV_DIM, EMBED_DIM), dtype=jnp.float32) * s, 'Wo': jax.random.normal(ks[4], (EMBED_DIM, EMBED_DIM), dtype=jnp.float32) * s}
    _L0_attn_in = _L0_attn_setup()

    def _L0_ffn_setup():
        import jax, jax.numpy as jnp
        import numpy as np
        TOP_P = 0.9
        S, B, H, I, E = (256, 4, 256, 512, 8)

        def _top_p_weights(probs, top_p):
            order = jnp.argsort(-probs, axis=-1)
            sp = jnp.take_along_axis(probs, order, axis=-1)
            cum = jnp.cumsum(sp, axis=-1)
            exceed = cum > top_p
            first_idx = jnp.argmax(exceed, axis=-1)
            first = jnp.arange(probs.shape[-1])[None, :] == first_idx[:, None]
            keep = ~exceed | first
            kept = jnp.where(keep, sp, 0.0)
            t_idx = jnp.arange(probs.shape[0])[:, None]
            return jnp.zeros_like(probs).at[t_idx, order].set(kept)
        key = jax.random.key(seed)
        ks = jax.random.split(key, 5)
        scale = 0.02
        return {'hidden_states': jax.random.normal(ks[0], (S, B, H), dtype=jnp.float32), 'router_w': jax.random.normal(ks[1], (E, H), dtype=jnp.float32) * scale, 'gate_w': jax.random.normal(ks[2], (E, I, H), dtype=jnp.float32) * scale, 'up_w': jax.random.normal(ks[3], (E, I, H), dtype=jnp.float32) * scale, 'down_w': jax.random.normal(ks[4], (E, H, I), dtype=jnp.float32) * scale}
    _L0_ffn_in = _L0_ffn_setup()
    _L0_c = _w((lambda *s: np.random.randn(*s).astype(np.float32) * 0.05)(4, 256))
    _L0_wmod = _w((lambda *s: np.random.randn(*s).astype(np.float32) * 0.05)(256, 6 * 256) * 256 ** (-0.5))
    _d = {'L0_attn_x': _L0_attn_in['x'], 'L0_attn_Wq': _L0_attn_in['Wq'], 'L0_attn_Wk': _L0_attn_in['Wk'], 'L0_attn_Wv': _L0_attn_in['Wv'], 'L0_attn_Wo': _L0_attn_in['Wo'], 'L0_ffn_router_w': _L0_ffn_in['router_w'], 'L0_ffn_gate_w': _L0_ffn_in['gate_w'], 'L0_ffn_up_w': _L0_ffn_in['up_w'], 'L0_ffn_down_w': _L0_ffn_in['down_w'], 'L0_c': _L0_c, 'L0_wmod': _L0_wmod}
    _x0 = _d['L0_attn_x']
    _d['L0_attn_x'] = jax.random.normal(jax.random.fold_in(jax.random.key(seed), 1), (4, 512, 256), dtype=_x0.dtype)
    del _x0
    return _d

def reference(L0_attn_x, L0_attn_Wq, L0_attn_Wk, L0_attn_Wv, L0_attn_Wo, L0_ffn_router_w, L0_ffn_gate_w, L0_ffn_up_w, L0_ffn_down_w, L0_c, L0_wmod):

    def _L0_attn_ref(x, Wq, Wk, Wv, Wo):
        import jax, jax.numpy as jnp
        import numpy as np
        EMBED_DIM = 256
        NUM_HEADS = 16
        NUM_KV_HEADS = 4
        HEAD_DIM = EMBED_DIM // NUM_HEADS
        KV_DIM = NUM_KV_HEADS * HEAD_DIM
        B, N = (2, 256)
        RMS_EPS = float(jnp.finfo(jnp.float32).eps)
        L2_EPS = 1e-12

        def _rms_norm(t):
            ms = jnp.mean(t * t, axis=-1, keepdims=True)
            return t * jax.lax.rsqrt(ms + RMS_EPS)
        Bb, Nn, C = x.shape
        scale = HEAD_DIM ** (-0.5)
        rep = NUM_HEADS // NUM_KV_HEADS
        q = jnp.einsum('bnc,oc->bno', x, Wq).reshape(Bb, Nn, NUM_HEADS, HEAD_DIM).transpose(0, 2, 1, 3)
        k = jnp.einsum('bnc,oc->bno', x, Wk).reshape(Bb, Nn, NUM_KV_HEADS, HEAD_DIM).transpose(0, 2, 1, 3)
        v = jnp.einsum('bnc,oc->bno', x, Wv).reshape(Bb, Nn, NUM_KV_HEADS, HEAD_DIM).transpose(0, 2, 1, 3)
        q = _rms_norm(q)
        k = _rms_norm(k)
        k = jnp.repeat(k, rep, axis=1)
        v = jnp.repeat(v, rep, axis=1)
        attn = jnp.einsum('bhqd,bhkd->bhqk', q, k) * scale
        attn = jax.nn.softmax(attn, axis=-1)
        y = jnp.einsum('bhqk,bhkd->bhqd', attn, v)
        vn = v / jnp.maximum(jnp.linalg.norm(v, axis=-1, keepdims=True), L2_EPS)
        y = y - jnp.sum(y * vn, axis=-1, keepdims=True) * vn
        y = y.transpose(0, 2, 1, 3).reshape(Bb, Nn, C)
        return jnp.einsum('bnc,oc->bno', y, Wo)

    def _L0_ffn_ref(hidden_states, router_w, gate_w, up_w, down_w):
        import jax, jax.numpy as jnp
        import numpy as np
        TOP_P = 0.9
        S, B, H, I, E = (256, 4, 256, 512, 8)

        def _top_p_weights(probs, top_p):
            order = jnp.argsort(-probs, axis=-1)
            sp = jnp.take_along_axis(probs, order, axis=-1)
            cum = jnp.cumsum(sp, axis=-1)
            exceed = cum > top_p
            first_idx = jnp.argmax(exceed, axis=-1)
            first = jnp.arange(probs.shape[-1])[None, :] == first_idx[:, None]
            keep = ~exceed | first
            kept = jnp.where(keep, sp, 0.0)
            t_idx = jnp.arange(probs.shape[0])[:, None]
            return jnp.zeros_like(probs).at[t_idx, order].set(kept)
        s, b, h = hidden_states.shape
        x = hidden_states.reshape(-1, h)
        probs = jax.nn.softmax(x @ router_w.T, axis=-1)
        w = _top_p_weights(probs, TOP_P)
        out = jnp.zeros_like(x)
        n_exp = router_w.shape[0]
        for e in range(n_exp):
            g = jax.nn.silu(x @ gate_w[e].T)
            u = x @ up_w[e].T
            y = g * u @ down_w[e].T
            out = out + y * w[:, e:e + 1]
        return out.reshape(s, b, h)
    x = L0_attn_x
    mod = (_silu(L0_c) @ L0_wmod).reshape(L0_c.shape[0], 6, 1, -1)
    sa, ca, ga, sb, cb, gb = (mod[:, 0], mod[:, 1], mod[:, 2], mod[:, 3], mod[:, 4], mod[:, 5])
    ga = (2 * (ga >= 0) - 1) * jnp.maximum(jnp.abs(ga), 0.25)
    gb = (2 * (gb >= 0) - 1) * jnp.maximum(jnp.abs(gb), 0.25)
    h = _layernorm(x, axis=-1) * (1 + ca) + sa
    x = x + ga * _L0_attn_ref(h, L0_attn_Wq, L0_attn_Wk, L0_attn_Wv, L0_attn_Wo)
    h = _layernorm(x, axis=-1) * (1 + cb) + sb
    x = x + gb * _L0_ffn_ref(h, L0_ffn_router_w, L0_ffn_gate_w, L0_ffn_up_w, L0_ffn_down_w)
    return x

_drawn_inputs = setup_inputs


def setup_inputs(seed=0):
    import zlib

    import numpy as np

    out = dict(_drawn_inputs(seed))
    spreads = {}
    factors = {'L0_attn_Wq': 3.025,
     'L0_attn_Wk': 3.022,
     'L0_ffn_router_w': 8.0,
     'L0_ffn_gate_w': 8.0,
     'L0_ffn_up_w': 8.0,
     'L0_ffn_down_w': 8.0}
    for name, (base, spread) in spreads.items():
        noise = np.random.default_rng([zlib.crc32(name.encode()), seed]).standard_normal(out[name].shape)
        drawn = base * np.exp(spread * noise) if base else spread * noise
        out[name] = jnp.asarray(drawn.astype(out[name].dtype))
    for name, factor in factors.items():
        out[name] = (out[name] * factor).astype(out[name].dtype)
    return out
```

```python
from contextlib import ExitStack

import concourse.bass as bass
import concourse.mybir as mybir

F32 = mybir.dt.float32
F32R = mybir.dt.float32r
BF16 = mybir.dt.bfloat16
ALU = mybir.AluOpType
ACT = mybir.ActivationFunctionType
AX = mybir.AxisListType

P = 128
LN_EPS = 1e-5
RMS_EPS = 1.1920928955078125e-07
L2_EPS_SQUARED = 1e-24
TOP_P = 0.9
GATE_LEAST = 0.25
SHIFT_A, SCALE_A, GATE_A, SHIFT_B, SCALE_B, GATE_B = range(6)


def adaln_block(nc, x, wqT, wkT, wvT, woT, routerT, gateT, upT, downT, cT, wmod, out):
    B, N, C = x.shape
    KC = C // P
    TT = N // P
    NT = B * TT
    T = B * N
    KV = wkT.shape[1]
    QKV = C + 2 * KV
    D = 16
    H = C // D
    G = KV // D
    R = H // G
    HG = H + G
    ALLH = H + 2 * G
    E, _, I = gateT.shape
    KI = I // P
    TERMS = 6
    QW = TERMS * D
    ATT_SCALE = float(D) ** -0.5
    UNITS = G * TT * 2
    YROWS = 32
    CH = N
    NCH = T // CH
    TPC = CH // P

    ctx = ExitStack()
    with ctx:
        def sb(name, shape, dt=F32):
            return ctx.enter_context(nc.sbuf_tensor(name, shape, dt))

        def sem(name):
            return ctx.enter_context(nc.semaphore(name))

        x_all = sb("x_all", [P, NT, C])
        h2_hi = sb("h2_hi", [P, KC, T], F32R)
        h2_lo = sb("h2_lo", [P, KC, T], F32R)
        logits = sb("logits", [P, NT, E])
        moe_w = sb("moe_w", [P, NT, E])
        gate_rows = sb("gate_rows", [P, 2 * B, C])
        mod_cols = sb("mod_cols", [P, 4, KC, B])
        ident = sb("ident", [P, P])
        ident_b = sb("ident_b", [P, P], BF16)
        minus_half = sb("minus_half", [P, TT * ALLH])
        w_in = [sb(f"w_in{n}", [P, I * KC]) for n in range(3)]
        w_hi = [[sb(f"w_hi0_{n}", [P, I * KC], F32R) for n in range(3)]]
        w_lo = [[sb(f"w_lo0_{n}", [P, I * KC], F32R) for n in range(3)]]
        idle = sb("idle", [P, 1])
        tie = sb("tie", [P, E, E])
        attention_only = ctx.enter_context(ExitStack())
        keep = ctx

        def sb(name, shape, dt=F32):
            return attention_only.enter_context(nc.sbuf_tensor(name, shape, dt))

        w_qkv = sb("w_qkv", [P, KC, QKV])
        w_o = sb("w_o", [P, KC, C])
        w_r = sb("w_r", [P, KC, E])
        w_mod = sb("w_mod", [P, KC, 6 * C])
        silu_c = sb("silu_c", [P, KC, B])
        silu_t = sb("silu_t", [P, KC, B])
        silu_wide = sb("silu_wide", [P, KC, B, P])
        stats = sb("stats", [P, TT, 6])
        mean_var = sb("mean_var", [P, TT, 2])
        rstd = sb("rstd", [P, TT])
        var_eps = sb("var_eps", [P, TT])
        idle_v = sb("idle_v", [P, 1])
        xhat = sb("xhat", [P, TT, C])
        hT = sb("hT", [P, KC, N])
        mods = sb("mods", [P, 4, KC])
        qkv = sb("qkv", [P, TT, QKV])
        squares = sb("squares", [P, QKV])
        norms = sb("norms", [P, TT, ALLH])
        rnorm = sb("rnorm", [P, TT, ALLH])
        qkn = sb("qkn", [P, HG * D])
        rest = sb("rest", [P, HG * D])
        q6 = sb("q6", [P, H, TERMS, D], BF16)
        k6 = sb("k6", [P, G, TERMS, D], BF16)
        vn = sb("vn", [P, TT, G, D])
        v_aug = sb("v_aug", [P, TT, G, YROWS])
        qT = sb("qT", [QW, H, N], BF16)
        kT = sb("kT", [QW, G, N], BF16)
        probs = sb("probs", [P, 3, R, N])
        yT = sb("yT", [P, 2, N])
        rden = sb("rden", [P, TT, R])
        yn = sb("yn", [P, TT, R, D])
        prod = sb("prod", [P, TT, R, D])
        dots = sb("dots", [P, TT, R])
        y_nat = sb("y_nat", [P, TT, C])
        att = sb("att", [P, C])

        attention_only.close()

        def sb(name, shape, dt=F32):
            return ctx.enter_context(nc.sbuf_tensor(name, shape, dt))

        w_hi.append([sb(f"w_hi1_{n}", [P, I * KC], F32R) for n in range(3)])
        w_lo.append([sb(f"w_lo1_{n}", [P, I * KC], F32R) for n in range(3)])
        a_hi = sb("a_hi", [P, 2, KI, CH], F32R)
        a_lo = sb("a_lo", [P, 2, KI, CH], F32R)
        a_full = sb("a_full", [P, 2, CH])
        silu_g = sb("silu_g", [P, 2, CH])
        acc = sb("acc", [P, NT, C])
        rt_max = sb("rt_max", [P, NT])
        rt_sum = sb("rt_sum", [P, NT])
        rt_p = sb("rt_p", [P, NT, E])
        rt_gt = sb("rt_gt", [P, NT, E, E])
        rt_ge = sb("rt_ge", [P, NT, E, E])
        rt_before = sb("rt_before", [P, NT, E])

        psS = ctx.enter_context(nc.psum_tensor("psS", [P, 2, 2, 512], F32))
        psY = ctx.enter_context(nc.psum_tensor("psY", [P, 2, 512], F32))
        psM = ctx.enter_context(nc.psum_tensor("psM", [P, 2, 512], F32))
        psM_b = psM[:, :, :].bitcast(BF16)

        c_in, x_in, wmod_in, wattn_in, y_out = map(sem, "c_in x_in wmod_in wattn_in y_out".split())
        w_loaded = [sem(f"w_loaded{n}") for n in range(3)]
        zeroed, consts, silu_step, silu_done, modc_ps, modc_done, modr_ps, gate_copied, gate_step, modr_done = map(
            sem, "zeroed consts silu_step silu_done modc_ps modc_done modr_ps gate_copied gate_step modr_done".split())
        (mods_done, bn_done, ln_stats, ln_eps, ln_rstd, xhat_done, xT_ps, hT_done, qkv_ps, qkv_sb, squared, sq_sum, norm_eps,
         rnorm_done, qkn_done, v_done, q_hi, rest_done, q_mid, split_done, tr_ps, trq_done, trk_done, tr_done, scores,
         probs_done, pv_done, y_ps, y_sb, yback_ps, rden_done, yn_done, prod_done, dots_done, along_done, y_done, yT2_ps,
         yT2_done, o_ps, o_gated, x2_done, h2f_done, h2hi_done, h2_done, logit_ps, logit_done) = map(sem, (
            "mods_done bn_done ln_stats ln_eps ln_rstd xhat_done xT_ps hT_done qkv_ps qkv_sb squared sq_sum norm_eps "
            "rnorm_done qkn_done v_done q_hi rest_done q_mid split_done tr_ps trq_done trk_done tr_done scores "
            "probs_done pv_done y_ps y_sb yback_ps rden_done yn_done prod_done dots_done along_done y_done yT2_ps "
            "yT2_done o_ps o_gated x2_done h2f_done h2hi_done h2_done logit_ps logit_done").split())
        idle_done, idle_v_done = sem("idle_done"), sem("idle_v_done")
        (rt_step, rt_exp, rt_mask, w_rounded, w_ready, gate_ps, up_ps, silu_ready, a_ready, a_rounded, a_split, down_ps,
         acc_done, acc_zero, out_step, out_ready) = map(sem, (
            "rt_step rt_exp rt_mask w_rounded w_ready gate_ps up_ps silu_ready a_ready a_rounded a_split down_ps "
            "acc_done acc_zero out_step out_ready").split())
        block = ctx.enter_context(nc.Block())

        def settle(pool, before):
            pool.wait_ge(idle_done, before)
            pool.tensor_tensor(idle[:, :], minus_half[:, 0:1], minus_half[:, 0:1], ALU.mult).then_inc(idle_done, 1)

        def settle_v(dve, before):
            dve.wait_ge(idle_v_done, before)
            dve.memset(idle_v[:, :], 0.0).then_inc(idle_v_done, 1)

        w_src = [w.rearrange("e (k p) n -> e p k n", p=P) for w in (gateT, upT, downT)]

        def bank(tt):
            return psS[:, tt // 2, tt % 2, :]

        def down_bank(n, tp):
            return (psY, psM)[n % 2][:, tp // 2, (tp % 2) * C:(tp % 2 + 1) * C]

        @block.sync
        def _(sp):
            sp.dma_start(silu_c[:, :, :], cT.rearrange("(k p) b -> p k b", p=P)).then_inc(c_in, 16)
            sp.dma_start(x_all[:, 0:TT, :], x[0].rearrange("(t p) c -> p t c", p=P)).then_inc(x_in, 16)
            sp.dma_start(w_mod[:, :, :], wmod.rearrange("(k p) n -> p k n", p=P)).then_inc(wmod_in, 16)
            for w, (a, z) in ((wqT, (0, C)), (wkT, (C, C + KV)), (wvT, (C + KV, QKV))):
                sp.dma_start(w_qkv[:, :, a:z], w.rearrange("(k p) n -> p k n", p=P)).then_inc(wattn_in, 16)
            sp.dma_start(w_o[:, :, :], woT.rearrange("(k p) n -> p k n", p=P)).then_inc(wattn_in, 16)
            sp.dma_start(w_r[:, :, :], routerT.rearrange("(k p) n -> p k n", p=P)).then_inc(wattn_in, 16)
            for b in range(1, B):
                sp.dma_start(x_all[:, b * TT:(b + 1) * TT, :],
                             x[b].rearrange("(t p) c -> p t c", p=P)).then_inc(x_in, 16)
            with sp.Fori(0, E) as e:
                sp.wait_ge(w_ready, e * 3)
                for n in range(3):
                    sp.dma_start(w_in[n][:, :].rearrange("p (k n) -> p k n", k=w_src[n].shape[2]),
                                 w_src[n][e]).then_inc(w_loaded[n], 16)
            for b in range(B):
                sp.wait_ge(out_ready, (b + 1) * TT)
                sp.dma_start(out[b].rearrange("(t p) c -> p t c", p=P), acc[:, b * TT:(b + 1) * TT, :]).then_inc(y_out, 16)
            sp.wait_ge(y_out, 16 * B)

        @block.gpsimd
        def _(pool):
            pool.memset(ident[:, :], 0.0).then_inc(zeroed, 1)
            pool.memset(ident_b[:, :], 0.0).then_inc(zeroed, 1)
            pool.memset(v_aug[:, :, :, D:YROWS], 0.0).then_inc(zeroed, 1)
            pool.memset(tie[:, :, :], 1.0).then_inc(zeroed, 1)
            pool.wait_ge(zeroed, 4)
            for m in (ident, ident_b):
                pool.affine_select(out=m[:, :], in_=m[:, :], compare_op=ALU.not_equal, fill=1.0, base=0,
                                   pattern=[[-1, P]], channel_multiplier=1).then_inc(consts, 1)
            pool.affine_select(out=tie[:, :, :], in_=tie[:, :, :], compare_op=ALU.is_gt, fill=0.0, base=0,
                               pattern=[[1, E], [-1, E]], channel_multiplier=0).then_inc(consts, 1)
            pool.memset(minus_half[:, :], -0.5).then_inc(consts, 1)
            pool.memset(v_aug[:, :, :, D:D + 1], 1.0).then_inc(consts, 1)
            pool.wait_ge(consts, 5)

            def layer_rstd(b, n):
                pool.wait_ge(ln_eps, b * 2 + n + 1)
                pool.tensor_tensor(rstd[:, :], var_eps[:, :], minus_half[:, 0:TT], ALU.pow).then_inc(ln_rstd, 1)

            def split_weights(e, half):
                for n in range(3):
                    pool.wait_ge(w_loaded[n], e * 16 + 16)
                    settle(pool, B * KC + e * 3 + n)
                    pool.tensor_copy(w_hi[half][n][:, :], w_in[n][:, :]).then_inc(w_rounded, 1)
                    pool.wait_ge(w_rounded, e * 3 + n + 1)
                    pool.tensor_tensor(w_lo[half][n][:, :], w_in[n][:, :], w_hi[half][n][:, :].bitcast(F32),
                                       ALU.subtract).then_inc(w_ready, 1)

            with pool.Fori(0, B) as b:
                layer_rstd(b, 0)
                pool.wait_ge(norm_eps, b * 2 + 2)
                pool.tensor_tensor(rnorm[:, :, :].rearrange("p t h -> p (t h)"),
                                   norms[:, :, :].rearrange("p t h -> p (t h)"),
                                   minus_half[:, :], ALU.pow).then_inc(rnorm_done, 1)
                layer_rstd(b, 1)
                for k in range(KC):
                    pool.wait_ge(h2f_done, b * KC + k + 1)
                    settle(pool, b * KC + k)
                    pool.tensor_copy(h2_hi[:, k, bass.ds(b * N, N)], hT[:, k, :]).then_inc(h2hi_done, 1)
            split_weights(0, 0)
            pool.wait_ge(logit_done, B)
            pool.memset(acc[:, :, :], 0.0).then_inc(acc_zero, 1)
            split_weights(1, 1)
            with pool.Fori(1, E // 2) as e2:
                for half in range(2):
                    pool.wait_ge(down_ps, (2 * e2 + half - 1) * NCH * 2)
                    split_weights(2 * e2 + half, half)

        @block.scalar
        def _(act):
            act.wait_ge(c_in, 16)
            act.activation(silu_t[:, :, :], silu_c[:, :, :], ACT.Exp, scale=-1.0).then_inc(silu_step, 1)

            def modulate(b, n):
                for k in range(KC):
                    act.wait_ge(xT_ps, (b * 2 + n) * KC + k + 1)
                    if k == 0 and n == 0:
                        act.wait_ge(mods_done, b + 1)
                        act.wait_ge(h2_done, b * KC)
                        act.wait_ge(logit_ps, b)
                    if k == 0 and n == 1:
                        act.wait_ge(qkv_ps, (b + 1) * TT)
                    act.activation(hT[:, k, :], psM[:, k, :], ACT.Identity, bias=mods[:, 2 * n, k:k + 1],
                                   scale=mods[:, 2 * n + 1, k:k + 1]).then_inc(h2f_done if n else hT_done, 1)

            with act.Fori(0, B) as b:
                modulate(b, 0)
                for tt in range(TT):
                    act.wait_ge(qkv_ps, b * TT + tt + 1)
                    if tt == 0:
                        act.wait_ge(v_done, b * TT * 2)
                    act.copy(qkv[:, tt, :], bank(tt)[:, 0:QKV]).then_inc(qkv_sb, 1)
                for tt in range(TT):
                    act.wait_ge(qkn_done, b * TT + tt + 1)
                    act.wait_ge(tr_ps, 3 * (b * TT + tt))
                    qn = qkn[:, 0:H * D].rearrange("p (h o d) -> p h o d", o=1, d=D)
                    kn = qkn[:, H * D:].rearrange("p (h o d) -> p h o d", o=1, d=D)
                    act.copy(q6[:, :, 0:3, :], qn.broadcast_to([P, H, 3, D])).then_inc(q_hi, 1)
                    act.copy(k6[:, :, 0:4:3, :], kn.broadcast_to([P, G, 2, D])).then_inc(q_hi, 1)
                    act.copy(k6[:, :, 5:6, :], kn).then_inc(q_hi, 1)
                    qr = rest[:, 0:H * D].rearrange("p (h o d) -> p h o d", o=1, d=D)
                    kr = rest[:, H * D:].rearrange("p (h o d) -> p h o d", o=1, d=D)
                    act.wait_ge(rest_done, 2 * (b * TT + tt + 1))
                    act.copy(q6[:, :, 3:5, :], qr.broadcast_to([P, H, 2, D])).then_inc(q_mid, 1)
                    act.copy(k6[:, :, 1:5:3, :], kr.broadcast_to([P, G, 2, D])).then_inc(q_mid, 1)
                    act.wait_ge(tr_ps, 3 * (b * TT + tt) + 2)
                    act.copy(qT[:, 8:16, tt * P:(tt + 1) * P],
                             psM_b[0:QW, 1, :].rearrange("p (h t) -> p h t", h=8)).then_inc(tr_done, 1)
                for u in range(UNITS):
                    gk, pair = u // 2, u % 2
                    act.wait_ge(scores, b * UNITS + u + 1)
                    if pair == 0:
                        act.wait_ge(pv_done, b * TT * G + (gk - 2 if gk >= 3 else 0))
                    act.activation(probs[:, gk % 3, 2 * pair:2 * pair + 2, :], psS[:, u % 2, :, :], ACT.Exp,
                                   scale=ATT_SCALE).then_inc(probs_done, 1)
                for k in range(KC):
                    act.wait_ge(yT2_ps, b * KC + k + 1)
                    act.copy(yT[:, k, :], psM[:, k, :]).then_inc(yT2_done, 1)
                modulate(b, 1)

            act.wait_ge(rt_step, 2)
            act.activation(rt_p[:, :, :], rt_p[:, :, :], ACT.Exp).then_inc(rt_exp, 1)
            with act.Fori(0, E) as e:
                for n in range(NCH):
                    for i in range(KI):
                        m = e * NCH * KI + n * KI + i
                        act.wait_ge(gate_ps, m + 1)
                        act.wait_ge(a_ready, m - 1) if n or i > 1 else act.wait_ge(a_ready, e * NCH * KI)
                        act.activation(silu_g[:, i % 2, :], psS[:, 0, i % 2, :], ACT.Silu).then_inc(silu_ready, 1)
                        act.wait_ge(a_ready, m + 1)
                        if i == 0:
                            act.wait_ge(down_ps, e * NCH * 2 + 2 * (n - 1)) if n >= 2 else act.wait_ge(down_ps, e * NCH * 2)
                        act.copy(a_hi[:, n % 2, i, :], a_full[:, i % 2, :]).then_inc(a_rounded, 1)

        @block.vector
        def _(dve):
            dve.wait_ge(silu_step, 1)
            dve.tensor_scalar(silu_t[:, :, :], silu_t[:, :, :], 1.0, None, ALU.add).then_inc(silu_step, 1)
            dve.wait_ge(silu_step, 2)
            dve.reciprocal(silu_t[:, :, :], silu_t[:, :, :]).then_inc(silu_step, 1)
            dve.wait_ge(silu_step, 3)
            dve.tensor_tensor(silu_c[:, :, :], silu_c[:, :, :], silu_t[:, :, :], ALU.mult).then_inc(silu_step, 1)
            dve.wait_ge(silu_step, 4)
            dve.tensor_copy(silu_wide[:, :, :, :], silu_c[:, :, :].rearrange("p k (b o) -> p k b o", o=1).broadcast_to(
                [P, KC, B, P])).then_inc(silu_done, 1)
            dve.wait_ge(modc_ps, 1)
            for n in range(4):
                dve.tensor_scalar(mod_cols[:, n, :, :], psM[:, 0, n * KC * B:(n + 1) * KC * B].rearrange(
                    "p (k b) -> p k b", b=B), float(n % 2), None, ALU.add).then_inc(modc_done, 1)
            for m in range(2 * B):
                sign, size = rest[:, 0:C], squares[:, 0:C]
                dve.wait_ge(modr_ps, m + 1)
                dve.tensor_copy(att[:, :], psY[:, m % 2, 0:C]).then_inc(gate_copied, 1)
                dve.wait_ge(gate_copied, m + 1)
                dve.tensor_scalar(size, att[:, :], -1.0, GATE_LEAST, ALU.mult, ALU.max).then_inc(gate_step, 1)
                dve.tensor_scalar(sign, att[:, :], 0.0, 2.0, ALU.is_ge, ALU.mult).then_inc(gate_step, 1)
                dve.wait_ge(gate_step, 3 * m + 2)
                dve.tensor_tensor(size, size, att[:, :], ALU.max).then_inc(gate_step, 1)
                dve.wait_ge(gate_step, 3 * m + 3)
                dve.scalar_tensor_tensor(out=gate_rows[:, m, :], in0=sign, scalar=1.0, in1=size,
                                         op0=ALU.subtract, op1=ALU.mult).then_inc(modr_done, 1)
            dve.wait_ge(modc_done, 4)
            dve.wait_ge(modr_done, 2 * B)
            dve.wait_ge(x_in, 16 * B)

            def x_tile(b, tt):
                return x_all[:, bass.ds(b * TT + tt, 1), :].rearrange("p o c -> p (o c)")

            def normalise(b, n):
                if n:
                    dve.wait_ge(x2_done, (b + 1) * TT)
                    settle_v(dve, b * 3 + 1)
                for tt in range(TT):
                    dve.bn_stats(stats[:, tt, :], x_tile(b, tt)).then_inc(bn_done, 1)
                dve.wait_ge(bn_done, (b * 2 + n + 1) * TT)
                settle_v(dve, b * 3 + 2 * n)
                for tt in range(TT):
                    dve.bn_aggr(mean_var[:, tt, :], stats[:, tt, :]).then_inc(ln_stats, 1)
                dve.wait_ge(ln_stats, (b * 2 + n + 1) * TT)
                dve.tensor_scalar(var_eps[:, :], mean_var[:, :, 1], LN_EPS, None, ALU.add).then_inc(ln_eps, 1)
                dve.wait_ge(ln_rstd, b * 2 + n + 1)
                for tt in range(TT):
                    dve.tensor_scalar(xhat[:, tt, :], x_tile(b, tt), mean_var[:, tt, 0:1], rstd[:, tt:tt + 1],
                                      ALU.subtract, ALU.mult).then_inc(xhat_done, 1)

            with dve.Fori(0, B) as b:
                dve.wait_ge(h2f_done, b * KC)
                dve.tensor_copy(mods[:, :, :], mod_cols[:, :, :, bass.ds(b, 1)].rearrange(
                    "p n k o -> p n (k o)")).then_inc(mods_done, 1)
                normalise(b, 0)
                for tt in range(TT):
                    dve.wait_ge(qkv_sb, b * TT + tt + 1)
                    dve.tensor_tensor(squares[:, :], qkv[:, tt, :], qkv[:, tt, :], ALU.mult).then_inc(squared, 1)
                    dve.wait_ge(squared, b * TT + tt + 1)
                    dve.tensor_reduce(norms[:, tt, :], squares[:, :].rearrange("p (h d) -> p h d", d=D), AX.X,
                                      ALU.add).then_inc(sq_sum, 1)
                    dve.wait_ge(sq_sum, b * TT + tt + 1)
                dve.tensor_scalar(norms[:, :, 0:HG], norms[:, :, 0:HG], 1.0 / D, RMS_EPS,
                                  ALU.mult, ALU.add).then_inc(norm_eps, 1)
                dve.tensor_scalar(norms[:, :, HG:ALLH], norms[:, :, HG:ALLH], L2_EPS_SQUARED, None,
                                  ALU.max).then_inc(norm_eps, 1)
                dve.wait_ge(rnorm_done, b + 1)
                for tt in range(TT):
                    m = b * TT + tt
                    rn = rnorm[:, tt, :].rearrange("p (h o) -> p h o", o=1)
                    dve.tensor_tensor(qkn[:, :].rearrange("p (h d) -> p h d", d=D),
                                      qkv[:, tt, 0:HG * D].rearrange("p (h d) -> p h d", d=D),
                                      rn[:, 0:HG, :].broadcast_to([P, HG, D]), ALU.mult).then_inc(qkn_done, 1)
                    v = qkv[:, tt, HG * D:].rearrange("p (h d) -> p h d", d=D)
                    dve.tensor_tensor(vn[:, tt, :, :], v, rn[:, HG:, :].broadcast_to([P, G, D]),
                                      ALU.mult).then_inc(v_done, 1)
                    if tt == 0:
                        dve.wait_ge(pv_done, b * TT * G)
                    dve.tensor_copy(v_aug[:, tt, :, 0:D], v).then_inc(v_done, 1)
                    qn = qkn[:, 0:H * D].rearrange("p (h d) -> p h d", d=D)
                    kn = qkn[:, H * D:].rearrange("p (h d) -> p h d", d=D)
                    qr = rest[:, 0:H * D].rearrange("p (h d) -> p h d", d=D)
                    kr = rest[:, H * D:].rearrange("p (h d) -> p h d", d=D)
                    dve.wait_ge(qkn_done, m + 1)
                    dve.wait_ge(q_hi, 3 * (m + 1))
                    dve.tensor_tensor(qr, qn, q6[:, :, 0, :], ALU.subtract).then_inc(rest_done, 1)
                    dve.tensor_tensor(kr, kn, k6[:, :, 0, :], ALU.subtract).then_inc(rest_done, 1)
                    dve.wait_ge(rest_done, 2 * (m + 1))
                    dve.wait_ge(q_mid, 2 * (m + 1))
                    dve.tensor_tensor(q6[:, :, 5, :], qr, q6[:, :, 3, :], ALU.subtract).then_inc(split_done, 1)
                    dve.tensor_tensor(k6[:, :, 2, :], kr, k6[:, :, 1, :], ALU.subtract).then_inc(split_done, 1)
                    dve.wait_ge(tr_ps, 3 * m + 1)
                    dve.tensor_copy(qT[:, 0:8, tt * P:(tt + 1) * P],
                                    psM_b[0:QW, 0, :].rearrange("p (h t) -> p h t", h=8)).then_inc(trq_done, 1)
                    dve.wait_ge(tr_ps, 3 * m + 3)
                    dve.tensor_copy(kT[:, :, tt * P:(tt + 1) * P],
                                    psM_b[0:QW, 0, 0:G * P].rearrange("p (h t) -> p h t", h=G)).then_inc(trk_done, 1)
                for g in range(G):
                    m = b * G + g
                    dve.wait_ge(pv_done, (m + 1) * TT)
                    dve.tensor_copy(yT[:, g % 2, :], psY[:, g % 2, :]).then_inc(y_sb, 1)
                    dve.wait_ge(yback_ps, m + 1)
                    back = psM[:, g % 2, :].rearrange("p (t r w) -> p t r w", t=TT, r=R)
                    dve.reciprocal(rden[:, :, :], back[:, :, :, D]).then_inc(rden_done, 1)
                    dve.wait_ge(rden_done, m + 1)
                    dve.tensor_tensor(yn[:, :, :, :], back[:, :, :, 0:D],
                                      rden[:, :, :].rearrange("p t (r o) -> p t r o", o=1).broadcast_to([P, TT, R, D]),
                                      ALU.mult).then_inc(yn_done, 1)
                    dve.wait_ge(yn_done, m + 1)
                    vb = vn[:, :, g:g + 1, :].broadcast_to([P, TT, R, D])
                    dve.tensor_tensor(prod[:, :, :, :], yn[:, :, :, :], vb, ALU.mult).then_inc(prod_done, 1)
                    dve.wait_ge(prod_done, m + 1)
                    dve.tensor_reduce(dots[:, :, :], prod[:, :, :, :], AX.X, ALU.add).then_inc(dots_done, 1)
                    dve.wait_ge(dots_done, m + 1)
                    dve.tensor_tensor(prod[:, :, :, :], vb,
                                      dots[:, :, :].rearrange("p t (r o) -> p t r o", o=1).broadcast_to([P, TT, R, D]),
                                      ALU.mult).then_inc(along_done, 1)
                    dve.wait_ge(along_done, m + 1)
                    dve.tensor_tensor(y_nat[:, :, g * R * D:(g + 1) * R * D].rearrange("p t (r d) -> p t r d", d=D),
                                      yn[:, :, :, :], prod[:, :, :, :], ALU.subtract).then_inc(y_done, 1)
                ga = gate_rows[:, bass.ds(b, 1), :].rearrange("p o c -> p (o c)")
                for tt in range(TT):
                    dve.wait_ge(o_ps, b * TT + tt + 1)
                    if tt:
                        dve.wait_ge(x2_done, b * TT + tt)
                    dve.tensor_tensor(att[:, :], bank(tt)[:, 0:C], ga, ALU.mult).then_inc(o_gated, 1)
                    dve.wait_ge(o_gated, b * TT + tt + 1)
                    dve.tensor_tensor(x_tile(b, tt), x_tile(b, tt), att[:, :], ALU.add).then_inc(x2_done, 1)
                normalise(b, 1)
                for k in range(KC):
                    dve.wait_ge(h2hi_done, b * KC + k + 1)
                    dve.tensor_tensor(h2_lo[:, k, bass.ds(b * N, N)], hT[:, k, :],
                                      h2_hi[:, k, bass.ds(b * N, N)].bitcast(F32), ALU.subtract).then_inc(h2_done, 1)
                dve.wait_ge(logit_ps, b + 1)
                dve.tensor_copy(logits[:, bass.ds(b * TT, TT), :],
                                psY[:, 0, 0:TT * E].rearrange("p (t e) -> p t e", e=E)).then_inc(logit_done, 1)

            dve.wait_ge(logit_done, B)
            dve.wait_ge(consts, 5)
            dve.tensor_reduce(rt_max[:, :], logits[:, :, :], AX.X, ALU.max).then_inc(rt_step, 1)
            dve.wait_ge(rt_step, 1)
            wide = lambda v: v.rearrange("p (t o) -> p t o", o=1).broadcast_to([P, NT, E])
            dve.tensor_tensor(rt_p[:, :, :], logits[:, :, :], wide(rt_max[:, :]), ALU.subtract).then_inc(rt_step, 1)
            dve.wait_ge(rt_exp, 1)
            dve.tensor_reduce(rt_sum[:, :], rt_p[:, :, :], AX.X, ALU.add).then_inc(rt_step, 1)
            dve.wait_ge(rt_step, 3)
            dve.reciprocal(rt_sum[:, :], rt_sum[:, :]).then_inc(rt_step, 1)
            dve.wait_ge(rt_step, 4)
            dve.tensor_tensor(rt_p[:, :, :], rt_p[:, :, :], wide(rt_sum[:, :]), ALU.mult).then_inc(rt_step, 1)
            dve.wait_ge(rt_step, 5)
            other = rt_p[:, :, :].rearrange("p t (o e) -> p t o e", o=1).broadcast_to([P, NT, E, E])
            own = rt_p[:, :, :].rearrange("p t (e o) -> p t e o", o=1).broadcast_to([P, NT, E, E])
            ties = tie[:, :, :].rearrange("p (o e) j -> p o e j", o=1).broadcast_to([P, NT, E, E])
            dve.tensor_tensor(rt_ge[:, :, :, :], other, own, ALU.is_ge).then_inc(rt_step, 1)
            dve.tensor_tensor(rt_gt[:, :, :, :], other, own, ALU.is_gt).then_inc(rt_step, 1)
            dve.wait_ge(rt_step, 7)
            dve.tensor_tensor(rt_ge[:, :, :, :], rt_ge[:, :, :, :], ties, ALU.mult).then_inc(rt_step, 1)
            dve.wait_ge(rt_step, 8)
            dve.tensor_tensor(rt_gt[:, :, :, :], rt_gt[:, :, :, :], rt_ge[:, :, :, :], ALU.max).then_inc(rt_step, 1)
            dve.wait_ge(rt_step, 9)
            dve.tensor_tensor(rt_gt[:, :, :, :], rt_gt[:, :, :, :], other, ALU.mult).then_inc(rt_step, 1)
            dve.wait_ge(rt_step, 10)
            dve.tensor_reduce(rt_before[:, :, :], rt_gt[:, :, :, :], AX.X, ALU.add).then_inc(rt_step, 1)
            dve.wait_ge(rt_step, 11)
            dve.scalar_tensor_tensor(out=moe_w[:, :, :], in0=rt_before[:, :, :], scalar=TOP_P, in1=rt_p[:, :, :],
                                     op0=ALU.is_le, op1=ALU.mult).then_inc(rt_step, 1)
            dve.wait_ge(rt_step, 12)
            dve.wait_ge(acc_zero, 1)

            def accumulate(e, n, before):
                for tp in range(TPC):
                    t = n * TPC + tp
                    dve.wait_ge(down_ps, 2 * before + tp // 2 + 1)
                    dve.scalar_tensor_tensor(
                        out=acc[:, t, :], in0=down_bank(n, tp), scalar=moe_w[:, t, bass.ds(e, 1)],
                        in1=acc[:, t, :], op0=ALU.mult, op1=ALU.add).then_inc(acc_done, 1)

            with dve.Fori(0, E) as e:
                dve.wait_ge(acc_done, e * NCH * TPC)
                for n in range(NCH):
                    for i in range(KI):
                        m = e * NCH * KI + n * KI + i
                        dve.wait_ge(silu_ready, m + 1)
                        dve.wait_ge(up_ps, m + 1)
                        dve.tensor_tensor(a_full[:, i % 2, :], psS[:, 1, i % 2, :], silu_g[:, i % 2, :],
                                          ALU.mult).then_inc(a_ready, 1)
                        dve.wait_ge(a_ready, m + 1)
                        dve.wait_ge(a_rounded, m + 1)
                        dve.tensor_tensor(a_lo[:, n % 2, i, :], a_full[:, i % 2, :],
                                          a_hi[:, n % 2, i, :].bitcast(F32), ALU.subtract).then_inc(a_split, 1)
                        if i == KI - 2 and n:
                            accumulate(e, n - 1, e * NCH + n - 1)
                accumulate(e, NCH - 1, e * NCH + NCH - 1)
            dve.wait_ge(acc_done, E * NCH * TPC)
            for t in range(NT):
                dve.tensor_tensor(acc[:, t, :], acc[:, t, :], gate_rows[:, B + t // TT, :], ALU.mult).then_inc(out_step, 1)
                dve.wait_ge(out_step, t + 1)
                dve.tensor_tensor(acc[:, t, :], acc[:, t, :], x_all[:, t, :], ALU.add).then_inc(out_ready, 1)

        @block.tensor
        def _(pe):
            pe.wait_ge(wmod_in, 16)
            pe.wait_ge(silu_step, 4)
            for n, m in enumerate((SHIFT_A, SCALE_A, SHIFT_B, SCALE_B)):
                for k in range(KC):
                    for j in range(KC):
                        mm = pe.matmul(psM[:, 0, (n * KC + k) * B:(n * KC + k + 1) * B],
                                       w_mod[:, j, m * C + k * P:m * C + (k + 1) * P], silu_c[:, j, :],
                                       start=j == 0, stop=j == KC - 1)
            mm.then_inc(modc_ps, 1)
            pe.wait_ge(silu_done, 1)
            for m in range(2 * B):
                if m >= 2:
                    pe.wait_ge(gate_copied, m - 1)
                at = (GATE_A, GATE_B)[m // B] * C
                for j in range(KC):
                    mm = pe.matmul(psY[:, m % 2, 0:C], silu_wide[:, j, m % B, :], w_mod[:, j, at:at + C],
                                   start=j == 0, stop=j == KC - 1)
                mm.then_inc(modr_ps, 1)
            pe.wait_ge(consts, 5)
            pe.wait_ge(modc_done, 4)
            pe.wait_ge(gate_copied, 2 * B)
            pe.wait_ge(wattn_in, 80)

            def turn_x(b, n):
                pe.wait_ge(xhat_done, (b * 2 + n + 1) * TT)
                pe.wait_ge(yT2_done, (b + 1) * KC) if n else pe.wait_ge(h2f_done, b * KC)
                for k in range(KC):
                    for tt in range(TT):
                        mm = pe.transpose(psM[:, k, tt * P:(tt + 1) * P], xhat[:, tt, k * P:(k + 1) * P], ident[:, :])
                    mm.then_inc(xT_ps, 1)

            def turn_heads(dst, src, heads):
                for j, h in enumerate(heads):
                    mm = pe.transpose(dst[0:QW, j * P:(j + 1) * P], src[:, h, :, :].rearrange("p a d -> p (a d)"),
                                      ident_b[:, :])
                return mm

            with pe.Fori(0, B) as b:
                turn_x(b, 0)
                pe.wait_ge(hT_done, (b + 1) * KC)
                pe.wait_ge(o_gated, b * TT)
                for tt in range(TT):
                    for k in range(KC):
                        mm = pe.matmul(bank(tt)[:, 0:QKV], hT[:, k, tt * P:(tt + 1) * P], w_qkv[:, k, :],
                                       start=k == 0, stop=k == KC - 1)
                    mm.then_inc(qkv_ps, 1)
                for tt in range(TT):
                    m = b * TT + tt
                    pe.wait_ge(split_done, 2 * (m + 1))
                    pe.wait_ge(q_hi, 3 * (m + 1))
                    if tt:
                        pe.wait_ge(trk_done, m)
                        pe.wait_ge(tr_done, m)
                    turn_heads(psM_b[:, 0, :], q6, range(0, 8)).then_inc(tr_ps, 1)
                    turn_heads(psM_b[:, 1, :], q6, range(8, 16)).then_inc(tr_ps, 1)
                    pe.wait_ge(trq_done, m + 1)
                    turn_heads(psM_b[:, 0, :], k6, range(G)).then_inc(tr_ps, 1)
                pe.wait_ge(trk_done, (b + 1) * TT)
                pe.wait_ge(tr_done, (b + 1) * TT)
                pe.wait_ge(v_done, 2 * (b + 1) * TT)

                def score(u):
                    gk, pair = u // 2, u % 2
                    g, kt = gk // TT, gk % TT
                    if u < 2:
                        pe.wait_ge(qkv_sb, (b + 1) * TT)
                    else:
                        pe.wait_ge(probs_done, b * UNITS + u - 1)
                    for j in range(2):
                        mm = pe.matmul(psS[:, u % 2, j, :], kT[:, g, kt * P:(kt + 1) * P],
                                       qT[:, g * R + 2 * pair + j, :], start=True, stop=True)
                    mm.then_inc(scores, 1)

                def turn_y(g):
                    pe.wait_ge(y_sb, b * G + g + 1)
                    if g >= 2:
                        pe.wait_ge(yn_done, b * G + g - 1)
                    for tt in range(TT):
                        mm = pe.transpose(psM[:, g % 2, tt * P:(tt + 1) * P], yT[:, g % 2, tt * P:(tt + 1) * P],
                                          ident[:, :])
                    mm.then_inc(yback_ps, 1)

                score(0)
                score(1)
                for gk in range(G * TT):
                    g, kt = gk // TT, gk % TT
                    if gk + 1 < G * TT:
                        score(2 * gk + 2)
                        score(2 * gk + 3)
                    if kt == 0:
                        pe.wait_ge(y_sb, b * G + (g - 1 if g >= 2 else 0))
                        pe.wait_ge(logit_done, b)
                    pe.wait_ge(probs_done, b * UNITS + 2 * gk + 2)
                    for r in range(R):
                        mm = pe.matmul(psY[r * YROWS:(r + 1) * YROWS, g % 2, :], v_aug[:, kt, g, :],
                                       probs[:, gk % 3, r, :], start=kt == 0, stop=kt == TT - 1)
                    mm.then_inc(pv_done, 1)
                    if kt == 1 and g:
                        turn_y(g - 1)
                turn_y(G - 1)
                pe.wait_ge(y_done, (b + 1) * G)
                for k in range(KC):
                    for tt in range(TT):
                        mm = pe.transpose(psM[:, k, tt * P:(tt + 1) * P], y_nat[:, tt, k * P:(k + 1) * P], ident[:, :])
                    mm.then_inc(yT2_ps, 1)
                pe.wait_ge(yT2_done, (b + 1) * KC)
                pe.wait_ge(probs_done, (b + 1) * UNITS)
                for tt in range(TT):
                    for k in range(KC):
                        mm = pe.matmul(bank(tt)[:, 0:C], yT[:, k, tt * P:(tt + 1) * P], w_o[:, k, :],
                                       start=k == 0, stop=k == KC - 1)
                    mm.then_inc(o_ps, 1)
                turn_x(b, 1)
                pe.wait_ge(h2f_done, (b + 1) * KC)
                pe.wait_ge(y_sb, (b + 1) * G)
                for tt in range(TT):
                    for k in range(KC):
                        mm = pe.matmul(psY[:, 0, tt * E:(tt + 1) * E], hT[:, k, tt * P:(tt + 1) * P], w_r[:, k, :],
                                       start=k == 0, stop=k == KC - 1)
                mm.then_inc(logit_ps, 1)

            pe.wait_ge(h2_done, B * KC)
            pe.wait_ge(o_gated, B * TT)
            pe.wait_ge(logit_done, B)

            def gate_up(e, half, n, i):
                m = e * NCH * KI + n * KI + i
                for part, (ps, ready) in enumerate(((psS[:, 0, i % 2, :], gate_ps), (psS[:, 1, i % 2, :], up_ps))):
                    used = silu_ready if part == 0 else a_ready
                    pe.wait_ge(used, e * NCH * KI if n == 0 and i < 2 else m - 1)
                    at = 0
                    for k in range(KC):
                        cols = slice(k * I + i * P, k * I + (i + 1) * P)
                        hi, lo = w_hi[half][part][:, cols], w_lo[half][part][:, cols]
                        tok = slice(n * CH, (n + 1) * CH)
                        for w, v in ((hi, h2_hi[:, k, tok]), (hi, h2_lo[:, k, tok]), (lo, h2_hi[:, k, tok])):
                            mm = pe.matmul(ps, w, v, start=at == 0, stop=at == 3 * KC - 1)
                            at += 1
                    mm.then_inc(ready, 1)

            def down(e, half, n):
                step = e * NCH + n
                pe.wait_ge(a_split, (step + 1) * KI)
                pe.wait_ge(acc_done, e * NCH * TPC if n < 2 else (step - 1) * TPC)
                for tp in range(TPC):
                    tok = slice(tp * P, (tp + 1) * P)
                    at = 0
                    for i in range(KI):
                        hi, lo = (w[half][2][:, i * C:(i + 1) * C] for w in (w_hi, w_lo))
                        for v, w in ((a_hi[:, n % 2, i, tok], hi), (a_hi[:, n % 2, i, tok], lo), (a_lo[:, n % 2, i, tok], hi)):
                            mm = pe.matmul(down_bank(n, tp), v, w, start=at == 0, stop=at == 3 * KI - 1)
                            at += 1
                    if tp % 2:
                        mm.then_inc(down_ps, 1)

            with pe.Fori(0, E // 2) as e2:
                for half in range(2):
                    e = 2 * e2 + half
                    pe.wait_ge(w_ready, 3 * e + 3)
                    for n in range(NCH):
                        for i in range(KI):
                            gate_up(e, half, n, i)
                            if i == 1 and n:
                                down(e, half, n - 1)
                    down(e, half, NCH - 1)


_INS = ["x", "wqT", "wkT", "wvT", "woT", "routerT", "gateT", "upT", "downT", "cT", "wmod"]


def kernel(L0_attn_x, L0_attn_Wq, L0_attn_Wk, L0_attn_Wv, L0_attn_Wo, L0_ffn_router_w, L0_ffn_gate_w, L0_ffn_up_w,
           L0_ffn_down_w, L0_c, L0_wmod):
    import concourse.bacc as bacc
    import numpy as np
    from concourse.bass_utils import run_bass_kernel_spmd

    turned = [np.swapaxes(w, -1, -2) for w in (L0_attn_Wq, L0_attn_Wk, L0_attn_Wv, L0_attn_Wo, L0_ffn_router_w,
                                               L0_ffn_gate_w, L0_ffn_up_w, L0_ffn_down_w, L0_c)]
    arrays = dict(zip(_INS, map(np.ascontiguousarray, [L0_attn_x, *turned, L0_wmod])))
    nc = bacc.Bacc("TRN2", target_bir_lowering=False, num_devices=1)
    args = [nc.dram_tensor(k, v.shape, mybir.dt.from_np(v.dtype), kind="ExternalInput").ap() for k, v in arrays.items()]
    out = nc.dram_tensor("out", arrays["x"].shape, mybir.dt.from_np(arrays["x"].dtype), kind="ExternalOutput").ap()
    adaln_block(nc, *args, out)
    return run_bass_kernel_spmd(nc, [arrays], core_ids=[0]).results[0]["out"]
```

```python
from contextlib import ExitStack

import concourse.bass as bass
import concourse.mybir as mybir

F32 = mybir.dt.float32
F32R = mybir.dt.float32r
BF16 = mybir.dt.bfloat16
I32 = mybir.dt.int32
ALU = mybir.AluOpType
ACT = mybir.ActivationFunctionType
AX = mybir.AxisListType

P = 128
LN_EPS = 1e-5
RMS_EPS = 1.1920928955078125e-07
L2_EPS_SQUARED = 1e-24
TOP_P = 0.9
GATE_LEAST = 0.25
SHIFT_A, SCALE_A, GATE_A, SHIFT_B, SCALE_B, GATE_B = range(6)


def adaln_block(nc, x, wqT, wkT, wvT, woT, routerT, gateT, upT, downT, cT, wmod, out):
    B, N, C = x.shape
    KC = C // P
    TT = N // P
    NT = B * TT
    T = B * N
    KV = wkT.shape[1]
    QKV = C + 2 * KV
    D = 16
    H = C // D
    G = KV // D
    R = H // G
    HG = H + G
    ALLH = H + 2 * G
    E, _, I = gateT.shape
    KI = I // P
    TERMS = 6
    QW = TERMS * D
    ATT_SCALE = float(D) ** -0.5
    UNITS = G * TT * 2
    YROWS = 32
    S = 2
    TSLOTS = T // P
    ITEMS = E * TSLOTS // S
    ROW = C + E
    PADS = S * P
    SW = S * P
    GATE_ROW, SHIFT_ROW, SCALE_ROW = 0, 2 * B, 3 * B

    ctx = ExitStack()
    with ctx:
        attention_only = ctx.enter_context(ExitStack())
        h_rows = nc.dram_tensor("h_rows", [T + PADS, ROW], F32)
        y_rows = nc.dram_tensor("y_rows", [T + PADS, C], F32)

        def sb(name, shape, dt=F32):
            return ctx.enter_context(nc.sbuf_tensor(name, shape, dt))

        def att(name, shape, dt=F32):
            return attention_only.enter_context(nc.sbuf_tensor(name, shape, dt))

        def sem(name):
            return ctx.enter_context(nc.semaphore(name))

        def sems(names):
            return [sem(n) for n in names.split()]

        x_all = sb("x_all", [P, NT, C])
        logits = sb("logits", [P, NT, E])
        moe_w = sb("moe_w", [P, NT, E])
        mod_rows = sb("mod_rows", [P, 4 * B, C])
        ident = sb("ident", [P, P])
        ident_b = sb("ident_b", [P, P], BF16)
        minus_half = sb("minus_half", [P, NT])
        zeros = sb("zeros", [P, ROW])
        idle = sb("idle", [P, 1])
        tie = sb("tie", [P, E, E])
        earlier = sb("earlier", [P, P], BF16)
        ones_b = sb("ones_b", [P, P], BF16)
        iota_row = sb("iota_row", [P, P])
        iota_tt = sb("iota_tt", [P, NT])
        part1 = sb("part1", [P, 1])
        pad_row = sb("pad_row", [P, 2, TSLOTS // 2])
        w_in = [sb(f"w_in{n}", [P, I * KC]) for n in range(3)]
        setup_only = ctx.enter_context(ExitStack())
        w_mod = setup_only.enter_context(nc.sbuf_tensor("w_mod", [P, KC, 6 * C], F32))
        silu_wide = setup_only.enter_context(nc.sbuf_tensor("silu_wide", [P, KC, B, P], F32))
        setup_only.close()
        w_hi, w_lo = ([[sb(f"{part}0_{n}", [P, I * KC], F32R) for n in range(3)]] for part in ("w_hi", "w_lo"))

        w_qkv = att("w_qkv", [P, KC, QKV])
        w_o = att("w_o", [P, KC, C])
        w_r = att("w_r", [P, KC, E])
        mod_cols = att("mod_cols", [P, 2, KC, B])
        silu_c = att("silu_c", [P, KC, B])
        silu_t = att("silu_t", [P, KC, B])
        stats1 = att("stats1", [P, NT, 6])
        mean_var1 = att("mean_var1", [P, NT, 2])
        var_eps1 = att("var_eps1", [P, NT])
        rstd1 = att("rstd1", [P, NT])
        stats = att("stats", [P, TT, 6])
        mean_var = att("mean_var", [P, TT, 2])
        var_eps = att("var_eps", [P, TT])
        rstd = att("rstd", [P, TT])
        idle_v = att("idle_v", [P, 1])
        xhat = att("xhat", [P, TT, C])
        h_nat = att("h_nat", [P, TT, C])
        hT = att("hT", [P, KC, N])
        mods = att("mods", [P, 2, KC])
        qkv = att("qkv", [P, TT, QKV])
        squares = att("squares", [P, QKV])
        norms = att("norms", [P, TT, ALLH])
        rnorm = att("rnorm", [P, TT, ALLH])
        newton = att("newton", [P, TT * ALLH])
        q6 = att("q6", [P, 2, H, TERMS, D], BF16)
        k6 = att("k6", [P, TT, G, TERMS, D], BF16)
        vn = att("vn", [P, 2, TT, G, D])
        v_aug = att("v_aug", [P, 2, TT, G, YROWS])
        qT = att("qT", [QW, 2, H, N], BF16)
        kT = att("kT", [QW, 2, G, N], BF16)
        probs = att("probs", [P, 4, R, N])
        yT = att("yT", [P, 2, N])
        rden = att("rden", [P, TT, R])
        yn = att("yn", [P, TT, R, D])
        prod = att("prod", [P, TT, R, D])
        dots = att("dots", [P, TT, R])
        y_nat = att("y_nat", [P, TT, C])
        row = att("row", [P, C])
        attention_only.close()

        for parts, part in ((w_hi, "w_hi"), (w_lo, "w_lo")):
            parts.append([sb(f"{part}1_{n}", [P, I * KC], F32R) for n in range(3)])
        rt_max = sb("rt_max", [P, NT])
        rt_sum = sb("rt_sum", [P, NT])
        rt_p = sb("rt_p", [P, NT, E])
        rt_gt = sb("rt_gt", [P, NT, E, E])
        rt_ge = sb("rt_ge", [P, NT, E, E])
        rt_before = sb("rt_before", [P, NT, E])
        keep = sb("keep", [P, NT, E])
        keep_b = sb("keep_b", [P, NT, E], BF16)
        rank = sb("rank", [P, NT, E])
        run = [sb(f"run{n}", [P, NT, E]) for n in range(2)]
        rank_i = sb("rank_i", [P, NT, E], I32)
        tile_i = sb("tile_i", [P, NT, E], I32)
        row_i = sb("row_i", [P, NT, E], I32)
        tile_f = sb("tile_f", [P, NT, E])
        row_f = sb("row_f", [P, NT, E])
        one_tile = sb("one_tile", [P, NT, E, TSLOTS])
        values = sb("values", [P, NT, E, 2, TSLOTS], BF16)
        one_row = sb("one_row", [P, 2, NT, P], BF16)
        lists = sb("lists", [P, E, 2, TSLOTS])
        ids = sb("ids", [P, E, TSLOTS])
        is_pad = sb("is_pad", [P, E, TSLOTS])
        ids_i = sb("ids_i", [P, E, TSLOTS], I32)
        idx_all = sb("idx_all", [P, S * ITEMS + 2 * TSLOTS], I32)
        cnt_i = sb("cnt_i", [P, E], I32)
        cnt_f = [sb(f"cnt_f{n}", [P, E]) for n in range(2)]
        items_f = sb("items_f", [P, E])
        meta = sb("meta", [P, 3, E], I32)
        idx_in = sb("idx_in", [P, S], I32)
        idx_out = sb("idx_out", [P, S], I32)
        h_sel = sb("h_sel", [P, S, ROW])
        hs_hi = sb("hs_hi", [P, KC, SW], F32R)
        hs_lo = sb("hs_lo", [P, KC, SW], F32R)
        w_sel = sb("w_sel", [P, ITEMS + TSLOTS, S, E + 1])
        silu_g = sb("silu_g", [P, 2, 2 * SW])
        a_full = sb("a_full", [P, 2, 2 * SW])
        a_hi = sb("a_hi", [P, KI, SW], F32R)
        a_lo = sb("a_lo", [P, KI, SW], F32R)
        y_sel = sb("y_sel", [P, S, C])
        y_all = sb("y_all", [P, NT, C])

        psS = ctx.enter_context(nc.psum_tensor("psS", [P, 2, 2, 512], F32))
        psY = ctx.enter_context(nc.psum_tensor("psY", [P, 2, 512], F32))
        psM = ctx.enter_context(nc.psum_tensor("psM", [P, 2, 512], F32))
        psM_b = psM[:, :, :].bitcast(BF16)

        c_in, wmod_in, wattn_in, x0_in, x_in, y_out = sems("c_in wmod_in wattn_in x0_in x_in y_out")
        w_loaded = [sem(f"w_loaded{n}") for n in range(3)]
        y_in = [sem(f"y_in{b}") for b in range(B)]
        zeroed, consts, silu_step, silu_done, modc_ps, modc_done, modr_ps, row_copied, gate_step, modr_done, idle_done = sems(
            "zeroed consts silu_step silu_done modc_ps modc_done modr_ps row_copied gate_step modr_done idle_done")
        (bn1_done, ln1_stats, ln1_eps, ln1_rstd, mods_done, xhat_done, xT_ps, hT_done, qkv_ps, qkv_sb, squared, sq_sum,
         newton_step, v_done, hi_done, rest_done, mid_done, lo_done, parts_done, q_turned, k_turned, trq_done, tr_done,
         trk_done) = sems(
            "bn1_done ln1_stats ln1_eps ln1_rstd mods_done xhat_done xT_ps hT_done qkv_ps qkv_sb squared sq_sum "
            "newton_step v_done hi_done rest_done mid_done lo_done parts_done q_turned k_turned trq_done tr_done "
            "trk_done")
        (scores, probs_done, pv_done, y_sb, yback_ps, rden_done, yn_done, prod_done, dots_done, along_done, y_done) = sems(
            "scores probs_done pv_done y_sb yback_ps rden_done yn_done prod_done dots_done along_done y_done")
        (yT2_ps, yT2_done, o_ps, o_gated, x2_done, idle_v_done, bn_done, ln_stats, ln_eps, ln_rstd, xhat2_done, h_scaled,
         h_done, h_out, h_turned, hT2_done, logit_ps, logit_done) = sems(
            "yT2_ps yT2_done o_ps o_gated x2_done idle_v_done bn_done ln_stats ln_eps ln_rstd xhat2_done h_scaled "
            "h_done h_out h_turned hT2_done logit_ps logit_done")
        rt_step, rt_exp, rt_kept, w_out, rank_ps, one_done, lists_ps, idx_ready, meta_ready = sems(
            "rt_step rt_exp rt_kept w_out rank_ps one_done lists_ps idx_ready meta_ready")
        (w_rounded, w_ready, gate_ps, up_ps, silu_ready, a_ready, a_rounded, a_split, down_ps, turned, sel_hi, sel_lo,
         w_copied, idx_copied, gathered, scattered, y_ready, out_step, out_ready) = sems(
            "w_rounded w_ready gate_ps up_ps silu_ready a_ready a_rounded a_split down_ps turned sel_hi sel_lo "
            "w_copied idx_copied gathered scattered y_ready out_step out_ready")
        block = ctx.enter_context(nc.Block())

        w_src = [w.rearrange("e (k p) n -> e p k n", p=P) for w in (gateT, upT, downT)]
        NCONST = 11
        FREE = 2
        SETTLED = 4

        def attention(eng, body):
            body(0, 0, True, False)
            with eng.Fori(0, (B - 2) // 2) as pair:
                body(2 * pair + 1, 1, True, True)
                body(2 * pair + 2, 0, True, True)
            body(B - 1, 1, False, True)

        def settle(pool, before):
            pool.wait_ge(idle_done, before + SETTLED)
            pool.tensor_tensor(idle[:, :], minus_half[:, 0:1], minus_half[:, 0:1], ALU.mult).then_inc(idle_done, 1)

        def settle_v(dve, before):
            dve.wait_ge(idle_v_done, before + 1)
            dve.memset(idle_v[:, :], 0.0).then_inc(idle_v_done, 1)

        def item_counts(eng, e):
            n = eng.value_load(meta[0:1, 0, bass.ds(e, 1)], min_val=1, max_val=TSLOTS // S)
            before = eng.value_load(meta[0:1, 1, bass.ds(e, 1)], min_val=0, max_val=ITEMS)
            return n, before

        def walk_items(eng, body, between):
            with eng.Fori(0, E // 2) as e2:
                for half in range(2):
                    e = 2 * e2 + half
                    n, before = item_counts(eng, e)
                    body(e, e2, True, before, half)
                    between(e, e2, half, before)
                    for i in range(1, 3):
                        with eng.If(n > i):
                            body(e, e2, False, before + i, half)
                    with eng.If(n > 3):
                        with eng.Fori(3, TSLOTS // S) as i:
                            with eng.If(n > i):
                                body(e, e2, False, before + i, half)

        ZEROING = 64

        @block.sync
        def _(sp):
            sp.sem_inc(h_out, 16)
            sp.dma_start(silu_c[:, :, :], cT.rearrange("(k p) b -> p k b", p=P)).then_inc(c_in, 16)
            sp.dma_start(x_all[:, 0:TT, :], x[0].rearrange("(t p) c -> p t c", p=P)).then_inc(x0_in, 16)
            sp.dma_start(w_mod[:, :, :], wmod.rearrange("(k p) n -> p k n", p=P)).then_inc(wmod_in, 16)
            for w, (a, z) in ((wqT, (0, C)), (wkT, (C, C + KV)), (wvT, (C + KV, QKV))):
                sp.dma_start(w_qkv[:, :, a:z], w.rearrange("(k p) n -> p k n", p=P)).then_inc(wattn_in, 16)
            sp.dma_start(w_o[:, :, :], woT.rearrange("(k p) n -> p k n", p=P)).then_inc(wattn_in, 16)
            sp.dma_start(w_r[:, :, :], routerT.rearrange("(k p) n -> p k n", p=P)).then_inc(wattn_in, 16)
            for b in range(1, B):
                sp.dma_start(x_all[:, b * TT:(b + 1) * TT, :],
                             x[b].rearrange("(t p) c -> p t c", p=P)).then_inc(x_in, 16)
            def load_weights(e):
                for n in range(3):
                    sp.dma_start(w_in[n][:, :].rearrange("p (k n) -> p k n", k=w_src[n].shape[2]),
                                 w_src[n][e]).then_inc(w_loaded[n], 16)

            load_weights(0)
            with sp.Fori(0, B) as b:
                sp.wait_ge(h_done, (b + 1) * TT)
                sp.dma_start(h_rows[bass.ds(b * N, N), 0:C].rearrange("(t p) c -> p t c", p=P),
                             h_nat[:, :, :]).then_inc(h_out, 16)
            sp.wait_ge(rt_kept, 1)
            sp.dma_start(h_rows[0:T, C:ROW].rearrange("(t p) e -> p t e", p=P), moe_w[:, :, :]).then_inc(w_out, 16)
            with sp.Fori(1, E) as e:
                sp.wait_ge(w_ready, e * 3)
                load_weights(e)
            sp.wait_ge(meta_ready, 1)
            items = sp.value_load(meta[0:1, 2, E - 1:E], min_val=E, max_val=ITEMS)
            sp.wait_ge(scattered, ZEROING + 32 * items)
            for b in range(B):
                sp.dma_start(y_all[:, b * TT:(b + 1) * TT, :],
                             y_rows[b * N:(b + 1) * N, :].rearrange("(t p) c -> p t c", p=P)).then_inc(y_in[b], 16)
            for b in range(B):
                sp.wait_ge(out_ready, (b + 1) * TT)
                sp.dma_start(out[b].rearrange("(t p) c -> p t c", p=P), y_all[:, b * TT:(b + 1) * TT, :]).then_inc(y_out, 16)
            sp.wait_ge(y_out, 16 * B)

        @block.gpsimd
        def _(pool):
            pool.sem_inc(idle_done, SETTLED)
            for m, v in ((ident, 0.0), (ident_b, 0.0), (v_aug[:, :, :, :, D:YROWS], 0.0), (tie, 1.0), (earlier, 1.0), (zeros, 0.0)):
                pool.memset(m[:] if m is not ident else m[:, :], v).then_inc(zeroed, 1)
            pool.wait_ge(zeroed, 6)
            for m in (ident, ident_b):
                pool.affine_select(out=m[:, :], in_=m[:, :], compare_op=ALU.not_equal, fill=1.0, base=0,
                                   pattern=[[-1, P]], channel_multiplier=1).then_inc(consts, 1)
            pool.affine_select(out=tie[:, :, :], in_=tie[:, :, :], compare_op=ALU.is_gt, fill=0.0, base=0,
                               pattern=[[1, E], [-1, E]], channel_multiplier=0).then_inc(consts, 1)
            pool.affine_select(out=earlier[:, :], in_=earlier[:, :], compare_op=ALU.is_gt, fill=0.0, base=0,
                               pattern=[[1, P]], channel_multiplier=-1).then_inc(consts, 1)
            pool.memset(ones_b[:, :], 1.0).then_inc(consts, 1)
            pool.memset(minus_half[:, :], -0.5).then_inc(consts, 1)
            pool.memset(v_aug[:, :, :, :, D:D + 1], 1.0).then_inc(consts, 1)
            small = dict(allow_small_or_imprecise_dtypes=True)
            pool.iota(iota_row[:, :], [[1, P]], base=0, channel_multiplier=0, **small).then_inc(consts, 1)
            pool.iota(iota_tt[:, :], [[1, NT]], base=0, channel_multiplier=0, **small).then_inc(consts, 1)
            pool.iota(part1[:, :], [[0, 1]], base=1, channel_multiplier=1, **small).then_inc(consts, 1)
            pool.iota(pad_row[:, :, :], [[P, 2], [0, TSLOTS // 2]], base=T, channel_multiplier=1, **small).then_inc(consts, 1)
            pool.wait_ge(consts, NCONST)
            for n, (a, z) in enumerate(((0, TT), (TT, NT))):
                pool.wait_ge(ln1_eps, n + 1)
                pool.tensor_tensor(rstd1[:, a:z], var_eps1[:, a:z], minus_half[:, 0:z - a], ALU.pow).then_inc(ln1_rstd, 1)
            for r0, r1 in ((0, T // 2), (T // 2, T), (T, T + PADS)):
                pool.dma_start(y_rows[r0:r1, :].rearrange("(t p) c -> p t c", p=P),
                               zeros[:, 0:C].rearrange("p (o c) -> p o c", o=1).broadcast_to([P, (r1 - r0) // P, C])
                               ).then_inc(scattered, 16)
            pool.dma_start(h_rows[T:T + PADS, :].rearrange("(t p) c -> p t c", p=P),
                           zeros[:, :].rearrange("p (o c) -> p o c", o=1).broadcast_to([P, S, ROW])).then_inc(scattered, 16)

            with pool.Fori(0, B) as b:
                pool.wait_ge(ln_eps, b + 1)
                pool.tensor_tensor(rstd[:, :], var_eps[:, :], minus_half[:, 0:TT], ALU.pow).then_inc(ln_rstd, 1)

            pool.wait_ge(h_out, 16 * (B + 1))
            pool.wait_ge(w_out, 16)
            pool.wait_ge(scattered, ZEROING)
            pool.wait_ge(idx_ready, E + 1)
            pool.wait_ge(meta_ready, 1)


            def gather(m, copied, settled):
                pool.tensor_copy(idx_in[:, :], idx_all[:, bass.ds(S * m, S)]).then_inc(idx_copied, 1)
                pool.wait_ge(idx_copied, copied)
                settle(pool, settled)
                for k in range(S):
                    pool.indirect_dma_start(h_sel[:, k, :], None, h_rows[:, :],
                                            bass.IndirectOffsetOnAxis(ap=idx_in[:, k:k + 1], axis=0)).then_inc(gathered, 16)

            def scatter(m, copied, settled):
                pool.wait_ge(y_ready, 2 * m + 2 + FREE)
                pool.wait_ge(scattered, ZEROING + 32 * m)
                settle(pool, settled)
                pool.tensor_copy(idx_out[:, :], idx_all[:, bass.ds(S * m, S)]).then_inc(idx_copied, 1)
                pool.wait_ge(idx_copied, copied)
                settle(pool, settled + 1)
                for k in range(S):
                    pool.indirect_dma_start(y_rows[:, :], bass.IndirectOffsetOnAxis(ap=idx_out[:, k:k + 1], axis=0),
                                            y_sel[:, k, :], None, compute_op=ALU.add).then_inc(scattered, 16)

            gather(0, 1, 0)
            for m in range(2):
                pool.wait_ge(turned, m + 1)
                pool.wait_ge(w_copied, m + 1)
                settle(pool, 2 * m + 1)
                gather(m + 1, m + 2, 2 * m + 2)
            items = pool.value_load(meta[0:1, 2, E - 1:E], min_val=E, max_val=ITEMS)
            with pool.Fori(0, ITEMS // 8) as some:
                with pool.If(items > 8 * some + 2):
                    with pool.Fori(2, 10) as nth:
                        m = 8 * some + nth
                        with pool.If(items > m):
                            pool.wait_ge(turned, m + 1)
                            pool.wait_ge(w_copied, m + 1)
                            settle(pool, SETTLED * m - 3)
                            gather(m + 1, 2 * m, SETTLED * m - 2)
                            scatter(m - 2, 2 * m + 1, SETTLED * m - 1)
            scatter(items - 2, 2 * items, SETTLED * items - 3)
            scatter(items - 1, 2 * items + 1, SETTLED * items - 1)

        @block.scalar
        def _(act):
            for freed, n in ((hT_done, 1), (hT2_done, 2 * KC), (probs_done, 2), (silu_ready, FREE)):
                act.sem_inc(freed, n)
            act.wait_ge(c_in, 16)
            act.activation(silu_t[:, :, :], silu_c[:, :, :], ACT.Exp, scale=-1.0).then_inc(silu_step, 1)


            def round_weights(e, half):
                for n in range(3):
                    act.wait_ge(w_loaded[n], e * 16 + 16)
                    act.copy(w_hi[half][n][:, :], w_in[n][:, :]).then_inc(w_rounded, 1)

            def scale_x(n):
                act.wait_ge(logit_ps, n + 1)
                act.wait_ge(mods_done, n + 1)
                for k in range(KC):
                    act.wait_ge(xT_ps, n * KC + k + 1)
                    act.activation(hT[:, k, :], psM[:, k, :], ACT.Identity, bias=mods[:, 0, k:k + 1],
                                   scale=mods[:, 1, k:k + 1]).then_inc(hT_done, 1)

            def take_qkv(n, tiles):
                for tt in tiles:
                    act.wait_ge(qkv_ps, n * TT + tt + 1)
                    if tt == 0:
                        act.wait_ge(lo_done, 2 * n * TT + 1)
                        act.wait_ge(v_done, 2 * n * TT + 1)
                    act.copy(qkv[:, tt, :], psM[:, tt % 2, 0:QKV]).then_inc(qkv_sb, 1)

            def repeat_parts(n, tt):
                act.wait_ge(hi_done, n * TT + tt + 1)
                act.wait_ge(mid_done, 2 * (n * TT + tt) + 2)
                q, k = q6[:, tt % 2, :, :, :], k6[:, tt, :, :, :]
                act.copy(q[:, :, 2:5:2, :], q[:, :, 0:1, :].broadcast_to([P, H, 2, D])).then_inc(parts_done, 1)
                act.copy(q[:, :, 3, :], q[:, :, 1, :]).then_inc(parts_done, 1)
                act.copy(k[:, :, 3:6:2, :], k[:, :, 0:1, :].broadcast_to([P, G, 2, D])).then_inc(parts_done, 1)
                act.copy(k[:, :, 2, :], k[:, :, 1, :]).then_inc(parts_done, 1)

            def take_q(n, parity, tt):
                act.wait_ge(q_turned, 2 * (n * TT + tt) + 2 + 4)
                act.copy(qT[:, parity, 8:16, tt * P:(tt + 1) * P],
                         psM_b[0:QW, 1, :].rearrange("p (h t) -> p h t", h=8)).then_inc(tr_done, 1)

            def take_y(p):
                act.wait_ge(logit_ps, p + 3)
                for k in range(KC):
                    act.wait_ge(yT2_ps, p * KC + k + 1 + KC)
                    act.copy(hT[:, k, :], psM[:, k, :]).then_inc(yT2_done, 1)

            def take_h(p, nth):
                k = KC - 1 - nth
                act.wait_ge(h_turned, p * KC + nth + 1)
                act.copy(hT[:, k, :], psM[:, k, :]).then_inc(hT2_done, 1)

            scale_x(0)
            take_qkv(0, range(TT))
            for m in range(4 * B):
                act.wait_ge(modr_ps, m + 1)
                act.copy(mod_rows[:, m, :], psY[:, m % 2, 0:C]).then_inc(row_copied, 1)
            for tiles in ((0, 1), (2, 3)):
                for tt in tiles:
                    repeat_parts(0, tt)
                for tt in tiles:
                    take_q(0, 0, tt)

            def body(b, parity, begin, end):
                for gk in range(G * TT):
                    for pair in range(2):
                        act.wait_ge(scores, b * UNITS + 2 * gk + pair + 1)
                        if pair == 0:
                            act.wait_ge(pv_done, b * TT * G + gk + 1)
                        act.activation(probs[:, gk % 4, 2 * pair:2 * pair + 2, :], psS[:, pair, :, :], ACT.Exp,
                                       scale=ATT_SCALE).then_inc(probs_done, 1)
                    if begin:
                        if gk == 1:
                            scale_x(b + 1)
                        elif gk == 3:
                            take_qkv(b + 1, (0, 1))
                        elif gk == 4:
                            take_qkv(b + 1, (2, 3))
                        elif gk in (6, 7, 9, 10):
                            repeat_parts(b + 1, {6: 0, 7: 1, 9: 2, 10: 3}[gk])
                        if gk in (8, 9, 11, 12):
                            take_q(b + 1, 1 - parity, {8: 0, 9: 1, 11: 2, 12: 3}[gk])
                    if end:
                        if gk == 5:
                            take_y(b - 1)
                        elif gk == 13:
                            take_h(b - 1, 0)
                        elif gk == 15:
                            take_h(b - 1, 1)
                    if not begin and gk == 8:
                        round_weights(0, 0)

            attention(act, body)
            take_y(B - 1)
            take_h(B - 1, 0)
            take_h(B - 1, 1)

            act.wait_ge(rt_step, 2)
            act.activation(rt_p[:, :, :], rt_p[:, :, :], ACT.Exp).then_inc(rt_exp, 1)

            def round_input(m):
                act.wait_ge(turned, m + 1)
                act.copy(hs_hi[:, :, :].rearrange("p k t -> p (k t)"), psM[:, 0, :]).then_inc(sel_hi, 1)

            def gate(m, h):
                act.wait_ge(gate_ps, 2 * m + h + 1)
                act.wait_ge(a_ready, 2 * m + h - 1 + FREE)
                act.activation(silu_g[:, h, :], psS[:, 0, h, :], ACT.Silu).then_inc(silu_ready, 1)

            def round_hidden(m, h):
                act.wait_ge(a_ready, 2 * m + h + 1 + FREE)
                act.wait_ge(down_ps, 2 * m + h - 1 + FREE)
                act.copy(a_hi[:, 2 * h:2 * h + 2, :].rearrange("p i t -> p (i t)"), a_full[:, h, :]).then_inc(a_rounded, 1)

            def body(e, e2, first, m, half):
                gate(m, 0)
                act.wait_ge(up_ps, 2 * m + 2)
                round_input(m + 1)
                round_hidden(m, 0)
                gate(m, 1)
                round_hidden(m, 1)

            def between_experts(e, e2, half, before):
                if half == 0:
                    act.wait_ge(down_ps, 2 * before + FREE)
                    round_weights(e + 1, 1)
                else:
                    with act.If(e2 < E // 2 - 1):
                        act.wait_ge(down_ps, 2 * before + FREE)
                        round_weights(e + 1, 0)

            act.wait_ge(meta_ready, 1)
            round_input(0)
            walk_items(act, body, between_experts)

        @block.vector
        def _(dve):
            for freed, n in ((v_done, 1), (lo_done, 1), (y_sb, 2), (yn_done, G), (idle_v_done, 1), (logit_done, 2), (a_ready, FREE),
                             (a_split, FREE), (y_ready, FREE)):
                dve.sem_inc(freed, n)
            dve.wait_ge(silu_step, 1)
            dve.tensor_scalar(silu_t[:, :, :], silu_t[:, :, :], 1.0, None, ALU.add).then_inc(silu_step, 1)
            dve.wait_ge(silu_step, 2)
            dve.reciprocal(silu_t[:, :, :], silu_t[:, :, :]).then_inc(silu_step, 1)
            dve.wait_ge(silu_step, 3)
            dve.tensor_tensor(silu_c[:, :, :], silu_c[:, :, :], silu_t[:, :, :], ALU.mult).then_inc(silu_step, 1)
            dve.wait_ge(silu_step, 4)
            dve.tensor_copy(silu_wide[:, :, :, :], silu_c[:, :, :].rearrange("p k (b o) -> p k b o", o=1).broadcast_to(
                [P, KC, B, P])).then_inc(silu_done, 1)
            def split_weights(e, half):
                for n in range(3):
                    dve.wait_ge(w_rounded, e * 3 + n + 1)
                    dve.tensor_tensor(w_lo[half][n][:, :], w_in[n][:, :], w_hi[half][n][:, :].bitcast(F32),
                                      ALU.subtract).then_inc(w_ready, 1)

            def x_tile(b, tt):
                return x_all[:, bass.ds(b * TT + tt, 1), :].rearrange("p o c -> p (o c)")

            def mean_and_variance(tiles):
                for t in tiles:
                    dve.bn_stats(stats1[:, t, :], x_all[:, t, :]).then_inc(bn1_done, 1)
                for t in tiles:
                    dve.wait_ge(bn1_done, t + 1)
                    dve.bn_aggr(mean_var1[:, t, :], stats1[:, t, :]).then_inc(ln1_stats, 1)
                dve.wait_ge(ln1_stats, tiles[-1] + 1)
                a, z = tiles[0], tiles[-1] + 1
                dve.tensor_scalar(var_eps1[:, a:z], mean_var1[:, a:z, 1], LN_EPS, None, ALU.add).then_inc(ln1_eps, 1)

            def modulate_gates():
                dve.wait_ge(row_copied, 4 * B)
                dve.wait_ge(xT_ps, 2 * KC)
                dve.tensor_scalar(mod_rows[:, 3 * B:4 * B, :], mod_rows[:, 3 * B:4 * B, :], 1.0, None,
                                  ALU.add).then_inc(modr_done, 1)
                size, sign = xhat, h_nat
                for n, g in enumerate((mod_rows[:, 0:B, :], mod_rows[:, B:2 * B, :])):
                    dve.tensor_scalar(size[:, :, :], g, -1.0, GATE_LEAST, ALU.mult, ALU.max).then_inc(gate_step, 1)
                    dve.tensor_scalar(sign[:, :, :], g, 0.0, 2.0, ALU.is_ge, ALU.mult).then_inc(gate_step, 1)
                    dve.wait_ge(gate_step, 3 * n + 2)
                    dve.tensor_tensor(size[:, :, :], size[:, :, :], g, ALU.max).then_inc(gate_step, 1)
                    dve.wait_ge(gate_step, 3 * n + 3)
                    dve.scalar_tensor_tensor(out=g, in0=sign[:, :, :], scalar=1.0, in1=size[:, :, :],
                                             op0=ALU.subtract, op1=ALU.mult).then_inc(modr_done, 1)
                    dve.wait_ge(modr_done, n + 2)

            def reciprocal_roots(b):
                dve.tensor_scalar(norms[:, :, 0:HG], norms[:, :, 0:HG], 1.0 / D, RMS_EPS,
                                  ALU.mult, ALU.add).then_inc(newton_step, 1)
                dve.tensor_scalar(norms[:, :, HG:ALLH], norms[:, :, HG:ALLH], L2_EPS_SQUARED, None,
                                  ALU.max).then_inc(newton_step, 1)
                z, y, t = (norms[:, :, :].rearrange("p t h -> p (t h)"), rnorm[:, :, :].rearrange("p t h -> p (t h)"),
                           newton[:, :])
                at = b * 13 + 2
                dve.wait_ge(newton_step, at)
                dve.tensor_scalar(t.bitcast(I32), z.bitcast(I32), 1, None, ALU.logical_shift_right).then_inc(newton_step, 1)
                dve.wait_ge(newton_step, at + 1)
                dve.tensor_scalar(y.bitcast(I32), t.bitcast(I32), -1.0, float(0x5f3759df), ALU.mult,
                                  ALU.add).then_inc(newton_step, 1)
                for step in range(3):
                    dve.wait_ge(newton_step, at + 3 * step + 2)
                    dve.tensor_tensor(t, y, y, ALU.mult).then_inc(newton_step, 1)
                    dve.wait_ge(newton_step, at + 3 * step + 3)
                    dve.scalar_tensor_tensor(out=t, in0=t, scalar=-0.5, in1=z, op0=ALU.mult, op1=ALU.mult).then_inc(newton_step, 1)
                    dve.wait_ge(newton_step, at + 3 * step + 4)
                    dve.scalar_tensor_tensor(out=y, in0=t, scalar=1.5, in1=y, op0=ALU.add, op1=ALU.mult).then_inc(newton_step, 1)
                dve.wait_ge(newton_step, at + 11)

            def normalise_x(n):
                dve.wait_ge(hT_done, n * KC + 1)
                dve.tensor_copy(mods[:, :, :], mod_cols[:, :, :, bass.ds(n, 1)].rearrange(
                    "p n k o -> p n (k o)")).then_inc(mods_done, 1)
                for tt in range(TT):
                    dve.tensor_scalar(xhat[:, tt, :], x_tile(n, tt),
                                      mean_var1[:, bass.ds(n * TT + tt, 1), 0:1].rearrange("p a b -> p (a b)"),
                                      rstd1[:, bass.ds(n * TT + tt, 1)], ALU.subtract, ALU.mult).then_inc(xhat_done, 1)

            def square_sums(n):
                for tt in range(TT):
                    dve.wait_ge(qkv_sb, n * TT + tt + 1)
                    dve.tensor_tensor(squares[:, :], qkv[:, tt, :], qkv[:, tt, :], ALU.mult).then_inc(squared, 1)
                    dve.wait_ge(squared, n * TT + tt + 1)
                    dve.tensor_reduce(norms[:, tt, :], squares[:, :].rearrange("p (h d) -> p h d", d=D), AX.X,
                                      ALU.add).then_inc(sq_sum, 1)
                    dve.wait_ge(sq_sum, n * TT + tt + 1)

            def split_heads(n, parity, tt):
                m = n * TT + tt
                rn = rnorm[:, tt, :].rearrange("p (h o) -> p h o", o=1)
                v = qkv[:, tt, HG * D:].rearrange("p (h d) -> p h d", d=D)
                qk = qkv[:, tt, 0:HG * D].rearrange("p (h d) -> p h d", d=D)
                q, k = q6[:, tt % 2, :, :, :], k6[:, tt, :, :, :]
                dve.wait_ge(q_turned, 2 * m + 2)
                dve.wait_ge(k_turned, 2 * n + tt // 2 + 1)
                dve.tensor_tensor(qk, qk, rn[:, 0:HG, :].broadcast_to([P, HG, D]), ALU.mult).then_inc(rest_done, 1)
                dve.tensor_tensor(vn[:, parity, tt, :, :], v, rn[:, HG:, :].broadcast_to([P, G, D]),
                                  ALU.mult).then_inc(v_done, 1)
                dve.tensor_copy(v_aug[:, parity, tt, :, 0:D], v).then_inc(v_done, 1)
                dve.wait_ge(rest_done, 3 * m + 1)
                dve.tensor_copy(q[:, :, 0, :], qk[:, 0:H, :]).then_inc(hi_done, 1)
                dve.tensor_copy(k[:, :, 0, :], qk[:, H:, :]).then_inc(hi_done, 1)
                dve.wait_ge(hi_done, 2 * m + 2)
                dve.tensor_tensor(qk[:, 0:H, :], qk[:, 0:H, :], q[:, :, 0, :], ALU.subtract).then_inc(rest_done, 1)
                dve.tensor_tensor(qk[:, H:, :], qk[:, H:, :], k[:, :, 0, :], ALU.subtract).then_inc(rest_done, 1)
                dve.wait_ge(rest_done, 3 * m + 3)
                dve.tensor_copy(q[:, :, 1, :], qk[:, 0:H, :]).then_inc(mid_done, 1)
                dve.tensor_copy(k[:, :, 1, :], qk[:, H:, :]).then_inc(mid_done, 1)
                dve.wait_ge(mid_done, 2 * m + 2)
                dve.tensor_tensor(q[:, :, 5, :], qk[:, 0:H, :], q[:, :, 1, :], ALU.subtract).then_inc(lo_done, 1)
                dve.tensor_tensor(k[:, :, 4, :], qk[:, H:, :], k[:, :, 1, :], ALU.subtract).then_inc(lo_done, 1)

            def take_q(n, parity, tt):
                dve.wait_ge(q_turned, 2 * (n * TT + tt) + 1 + 4)
                dve.tensor_copy(qT[:, parity, 0:8, tt * P:(tt + 1) * P],
                                psM_b[0:QW, 0, :].rearrange("p (h t) -> p h t", h=8)).then_inc(trq_done, 1)

            def take_k(n, parity, pair):
                dve.wait_ge(k_turned, 2 * n + pair + 1 + 2)
                dve.tensor_copy(kT[:, parity, :, 2 * pair * P:2 * (pair + 1) * P],
                                psM_b[0:QW, 0, :].rearrange("p (h t) -> p h t", h=G)).then_inc(trk_done, 1)

            def take_sums(b, g):
                dve.wait_ge(pv_done, b * TT * G + (g + 1) * TT + 4)
                dve.tensor_copy(yT[:, g % 2, :], psY[:, g % 2, :]).then_inc(y_sb, 1)

            def finish_y(b, parity, g):
                m = b * G + g
                dve.wait_ge(yback_ps, m + 1)
                back = psM[:, g % 2, :].rearrange("p (t r w) -> p t r w", t=TT, r=R)
                dve.reciprocal(rden[:, :, :], back[:, :, :, D]).then_inc(rden_done, 1)
                dve.wait_ge(rden_done, m + 1)
                dve.tensor_tensor(yn[:, :, :, :], back[:, :, :, 0:D],
                                  rden[:, :, :].rearrange("p t (r o) -> p t r o", o=1).broadcast_to([P, TT, R, D]),
                                  ALU.mult).then_inc(yn_done, 1)
                dve.wait_ge(yn_done, m + 1 + G)
                vb = vn[:, parity, :, g:g + 1, :].broadcast_to([P, TT, R, D])
                dve.tensor_tensor(prod[:, :, :, :], yn[:, :, :, :], vb, ALU.mult).then_inc(prod_done, 1)
                dve.wait_ge(prod_done, m + 1)
                dve.tensor_reduce(dots[:, :, :], prod[:, :, :, :], AX.X, ALU.add).then_inc(dots_done, 1)
                dve.wait_ge(dots_done, m + 1)
                dve.tensor_tensor(prod[:, :, :, :], vb,
                                  dots[:, :, :].rearrange("p t (r o) -> p t r o", o=1).broadcast_to([P, TT, R, D]),
                                  ALU.mult).then_inc(along_done, 1)
                dve.wait_ge(along_done, m + 1)
                if g == 0:
                    dve.wait_ge(yT2_ps, (b + 1) * KC)
                dve.tensor_tensor(y_nat[:, :, g * R * D:(g + 1) * R * D].rearrange("p t (r d) -> p t r d", d=D),
                                  yn[:, :, :, :], prod[:, :, :, :], ALU.subtract).then_inc(y_done, 1)

            def add_attention(p):
                ga = mod_rows[:, bass.ds(p, 1), :].rearrange("p o c -> p (o c)")
                for tt in range(TT):
                    dve.wait_ge(o_ps, 2 * p + tt // 2 + 1)
                    if tt:
                        dve.wait_ge(x2_done, p * TT + tt)
                    dve.tensor_tensor(row[:, :], psM[:, tt // 2, (tt % 2) * C:(tt % 2 + 1) * C], ga,
                                      ALU.mult).then_inc(o_gated, 1)
                    dve.wait_ge(o_gated, p * TT + tt + 1)
                    dve.tensor_tensor(x_tile(p, tt), x_tile(p, tt), row[:, :], ALU.add).then_inc(x2_done, 1)
                dve.wait_ge(x2_done, (p + 1) * TT)
                settle_v(dve, 2 * p)
                for tt in range(TT):
                    dve.bn_stats(stats[:, tt, :], x_tile(p, tt)).then_inc(bn_done, 1)
                dve.wait_ge(bn_done, (p + 1) * TT)
                settle_v(dve, 2 * p + 1)
                for tt in range(TT):
                    dve.bn_aggr(mean_var[:, tt, :], stats[:, tt, :]).then_inc(ln_stats, 1)
                dve.wait_ge(ln_stats, (p + 1) * TT)
                dve.tensor_scalar(var_eps[:, :], mean_var[:, :, 1], LN_EPS, None, ALU.add).then_inc(ln_eps, 1)

            def experts_input(p, begin):
                dve.wait_ge(ln_rstd, p + 1)
                if begin:
                    dve.wait_ge(xT_ps, (p + 3) * KC)
                for tt in range(TT):
                    dve.tensor_scalar(xhat[:, tt, :], x_tile(p, tt), mean_var[:, tt, 0:1], rstd[:, tt:tt + 1],
                                      ALU.subtract, ALU.mult).then_inc(xhat2_done, 1)
                scale_row, shift_row = (mod_rows[:, bass.ds(at + p, 1), :].rearrange("p o c -> p (o c)")
                                        for at in (SCALE_ROW, SHIFT_ROW))
                for tt in range(TT):
                    dve.wait_ge(xhat2_done, p * TT + tt + 1)
                    dve.tensor_tensor(xhat[:, tt, :], xhat[:, tt, :], scale_row, ALU.mult).then_inc(h_scaled, 1)
                dve.wait_ge(h_out, 16 * p + 16)
                for tt in range(TT):
                    dve.wait_ge(h_scaled, p * TT + tt + 1)
                    dve.tensor_tensor(h_nat[:, tt, :], xhat[:, tt, :], shift_row, ALU.add).then_inc(h_done, 1)

            def take_logits(p):
                dve.wait_ge(logit_ps, p + 1 + 3)
                dve.tensor_copy(logits[:, bass.ds(p * TT, TT), :],
                                psM[:, 1, 0:TT * E].rearrange("p (t e) -> p t e", e=E)).then_inc(logit_done, 1)

            dve.wait_ge(x0_in, 16)
            mean_and_variance(range(TT))
            dve.wait_ge(modc_ps, 1)
            for n in range(2):
                dve.tensor_scalar(mod_cols[:, n, :, :], psM[:, 0, n * KC * B:(n + 1) * KC * B].rearrange(
                    "p (k b) -> p k b", b=B), float(n % 2), None, ALU.add).then_inc(modc_done, 1)
            dve.wait_ge(modc_done, 2)
            dve.wait_ge(ln1_rstd, 1)
            normalise_x(0)
            square_sums(0)
            reciprocal_roots(0)
            split_heads(0, 0, 0)
            split_heads(0, 0, 1)
            dve.wait_ge(x_in, 16 * (B - 1))
            mean_and_variance(range(TT, NT))
            take_q(0, 0, 0)
            split_heads(0, 0, 2)
            take_q(0, 0, 1)
            split_heads(0, 0, 3)
            take_k(0, 0, 0)
            take_q(0, 0, 2)
            take_q(0, 0, 3)
            take_k(0, 0, 1)
            dve.wait_ge(ln1_rstd, 2)

            def body(b, parity, begin, end):
                if begin:
                    normalise_x(b + 1)
                if end:
                    take_sums(b - 1, G - 1)
                    finish_y(b - 1, 1 - parity, G - 1)
                if begin:
                    square_sums(b + 1)
                    reciprocal_roots(b + 1)
                take_sums(b, 0)
                if begin:
                    split_heads(b + 1, 1 - parity, 0)
                    split_heads(b + 1, 1 - parity, 1)
                finish_y(b, parity, 0)
                if end:
                    add_attention(b - 1)
                else:
                    modulate_gates()
                if begin:
                    take_q(b + 1, 1 - parity, 0)
                    split_heads(b + 1, 1 - parity, 2)
                    take_q(b + 1, 1 - parity, 1)
                take_sums(b, 1)
                if begin:
                    take_k(b + 1, 1 - parity, 0)
                    split_heads(b + 1, 1 - parity, 3)
                else:
                    split_weights(0, 0)
                finish_y(b, parity, 1)
                if end:
                    experts_input(b - 1, begin)
                if begin:
                    take_q(b + 1, 1 - parity, 2)
                    take_q(b + 1, 1 - parity, 3)
                take_sums(b, 2)
                if begin:
                    take_k(b + 1, 1 - parity, 1)
                finish_y(b, parity, 2)
                if end:
                    take_logits(b - 1)

            attention(dve, body)
            take_sums(B - 1, G - 1)
            finish_y(B - 1, (B - 1) % 2, G - 1)
            add_attention(B - 1)
            experts_input(B - 1, False)
            take_logits(B - 1)

            dve.wait_ge(logit_done, B + 2)
            dve.wait_ge(consts, NCONST)
            dve.tensor_reduce(rt_max[:, :], logits[:, :, :], AX.X, ALU.max).then_inc(rt_step, 1)
            dve.wait_ge(rt_step, 1)
            wide = lambda v: v.rearrange("p (t o) -> p t o", o=1).broadcast_to([P, NT, E])
            dve.tensor_tensor(rt_p[:, :, :], logits[:, :, :], wide(rt_max[:, :]), ALU.subtract).then_inc(rt_step, 1)
            dve.wait_ge(rt_exp, 1)
            dve.tensor_reduce(rt_sum[:, :], rt_p[:, :, :], AX.X, ALU.add).then_inc(rt_step, 1)
            dve.wait_ge(rt_step, 3)
            dve.reciprocal(rt_sum[:, :], rt_sum[:, :]).then_inc(rt_step, 1)
            dve.wait_ge(rt_step, 4)
            dve.tensor_tensor(rt_p[:, :, :], rt_p[:, :, :], wide(rt_sum[:, :]), ALU.mult).then_inc(rt_step, 1)
            dve.wait_ge(rt_step, 5)
            other = rt_p[:, :, :].rearrange("p t (o e) -> p t o e", o=1).broadcast_to([P, NT, E, E])
            own = rt_p[:, :, :].rearrange("p t (e o) -> p t e o", o=1).broadcast_to([P, NT, E, E])
            ties = tie[:, :, :].rearrange("p (o e) j -> p o e j", o=1).broadcast_to([P, NT, E, E])
            dve.tensor_tensor(rt_ge[:, :, :, :], other, own, ALU.is_ge).then_inc(rt_step, 1)
            dve.tensor_tensor(rt_gt[:, :, :, :], other, own, ALU.is_gt).then_inc(rt_step, 1)
            dve.wait_ge(rt_step, 7)
            dve.tensor_tensor(rt_ge[:, :, :, :], rt_ge[:, :, :, :], ties, ALU.mult).then_inc(rt_step, 1)
            dve.wait_ge(rt_step, 8)
            dve.tensor_tensor(rt_gt[:, :, :, :], rt_gt[:, :, :, :], rt_ge[:, :, :, :], ALU.max).then_inc(rt_step, 1)
            dve.wait_ge(rt_step, 9)
            dve.tensor_tensor(rt_gt[:, :, :, :], rt_gt[:, :, :, :], other, ALU.mult).then_inc(rt_step, 1)
            dve.wait_ge(rt_step, 10)
            dve.tensor_reduce(rt_before[:, :, :], rt_gt[:, :, :, :], AX.X, ALU.add).then_inc(rt_step, 1)
            dve.wait_ge(rt_step, 11)
            dve.tensor_scalar(keep[:, :, :], rt_before[:, :, :], TOP_P, None, ALU.is_le).then_inc(rt_step, 1)
            dve.wait_ge(rt_step, 12)
            dve.tensor_tensor(moe_w[:, :, :], keep[:, :, :], rt_p[:, :, :], ALU.mult).then_inc(rt_kept, 1)
            dve.tensor_copy(keep_b[:, :, :], keep[:, :, :]).then_inc(rt_kept, 1)

            at = [12]

            def step(ins):
                at[0] += 1
                ins.then_inc(rt_step, 1)
                dve.wait_ge(rt_step, at[0])

            dve.wait_ge(rank_ps, 1)
            tiles = psM[:, 1, 0:NT * E].rearrange("p (t e) -> p t e", e=E)
            step(dve.tensor_copy(run[0][:, :, :], tiles))
            hop = 1
            while hop < NT:
                old, new = run
                dve.tensor_copy(new[:, 0:hop, :], old[:, 0:hop, :]).then_inc(rt_step, 1)
                at[0] += 1
                step(dve.tensor_tensor(new[:, hop:, :], old[:, hop:, :], old[:, 0:NT - hop, :], ALU.add))
                run.reverse()
                hop *= 2
            total = run[0]
            step(dve.tensor_copy(rank[:, :, :], psM[:, 0, 0:NT * E].rearrange("p (t e) -> p t e", e=E)))
            step(dve.tensor_tensor(rank[:, 1:, :], rank[:, 1:, :], total[:, 0:NT - 1, :], ALU.add))
            step(dve.tensor_copy(rank_i[:, :, :], rank[:, :, :]))
            step(dve.tensor_scalar(tile_i[:, :, :], rank_i[:, :, :], 7, None, ALU.logical_shift_right))
            step(dve.tensor_scalar(row_i[:, :, :], rank_i[:, :, :], P - 1, None, ALU.bitwise_and))
            step(dve.tensor_copy(tile_f[:, :, :], tile_i[:, :, :]))
            step(dve.tensor_copy(row_f[:, :, :], row_i[:, :, :]))
            step(dve.scalar_tensor_tensor(out=row_f[:, :, :], in0=row_f[:, :, :], scalar=1.0, in1=keep[:, :, :],
                                          op0=ALU.add, op1=ALU.mult))
            step(dve.tensor_scalar(row_f[:, :, :], row_f[:, :, :], -1.0, None, ALU.add))
            dve.wait_ge(h_out, 16 * (B + 1))
            step(dve.tensor_tensor(one_tile[:, :, :, :], iota_row[:, 0:TSLOTS].rearrange("p (a o s) -> p a o s", a=1, o=1)
                                   .broadcast_to([P, NT, E, TSLOTS]),
                                   tile_f[:, :, :].rearrange("p t (e o) -> p t e o", o=1).broadcast_to([P, NT, E, TSLOTS]),
                                   ALU.is_equal))
            dve.tensor_scalar(values[:, :, :, 0, :], one_tile[:, :, :, :], part1[:, 0:1], None, ALU.mult).then_inc(rt_step, 1)
            at[0] += 1
            step(dve.tensor_tensor(values[:, :, :, 1, :], one_tile[:, :, :, :],
                                   iota_tt[:, :].rearrange("p (t o q) -> p t o q", o=1, q=1).broadcast_to([P, NT, E, TSLOTS]),
                                   ALU.mult))
            for e in range(E):
                if e >= 2:
                    dve.wait_ge(lists_ps, e - 1)
                dve.tensor_tensor(one_row[:, e % 2, :, :], iota_row[:, :].rearrange("p (o s) -> p o s", o=1)
                                  .broadcast_to([P, NT, P]),
                                  row_f[:, :, e:e + 1].broadcast_to([P, NT, P]), ALU.is_equal).then_inc(one_done, 1)
            step(dve.tensor_copy(cnt_i[:, :], total[:, NT - 1, :]))
            step(dve.tensor_scalar(items_f[:, :], cnt_i[:, :], float(SW - 1), None, ALU.add))
            step(dve.tensor_copy(cnt_i[:, :], items_f[:, :]))
            step(dve.tensor_scalar(meta[:, 0, :], cnt_i[:, :], 8, None, ALU.logical_shift_right))
            step(dve.tensor_scalar(meta[:, 0, :], meta[:, 0, :], 1.0, None, ALU.max))
            step(dve.tensor_copy(items_f[:, :], meta[:, 0, :]))
            step(dve.tensor_copy(cnt_f[0][:, :], items_f[:, :]))
            hop = 1
            while hop < E:
                old, new = cnt_f
                dve.tensor_copy(new[:, 0:hop], old[:, 0:hop]).then_inc(rt_step, 1)
                at[0] += 1
                step(dve.tensor_tensor(new[:, hop:], old[:, hop:], old[:, 0:E - hop], ALU.add))
                cnt_f.reverse()
                hop *= 2
            step(dve.tensor_copy(meta[:, 2, :], cnt_f[0][:, :]))
            step(dve.tensor_tensor(items_f[:, :], cnt_f[0][:, :], items_f[:, :], ALU.subtract))
            dve.tensor_copy(meta[:, 1, :], items_f[:, :]).then_inc(meta_ready, 1)
            dve.wait_ge(lists_ps, E)
            step(dve.tensor_copy(lists[:, :, :, :], psY[:, 0, 0:E * 2 * TSLOTS].rearrange("p (e v s) -> p e v s", e=E, v=2)))
            dve.scalar_tensor_tensor(out=ids[:, :, :], in0=lists[:, :, 1, :], scalar=float(P), in1=lists[:, :, 0, :],
                                     op0=ALU.mult, op1=ALU.add).then_inc(rt_step, 1)
            at[0] += 1
            step(dve.tensor_scalar(is_pad[:, :, :], lists[:, :, 0, :], 0.0, None, ALU.is_equal))
            pads = pad_row[:, :, :].rearrange("p k (o s) -> p o s k", o=1)
            dve.tensor_scalar(ids[:, :, :], ids[:, :, :], -1.0, None, ALU.add).then_inc(rt_step, 1)
            at[0] += 1
            pads1 = pad_row[:, :, :].rearrange("p k s -> p s k")
            for e in range(E):
                step(dve.scalar_tensor_tensor(out=is_pad[:, e, :].rearrange("p (s k) -> p s k", k=2), in0=pads1, scalar=1.0,
                                              in1=is_pad[:, e, :].rearrange("p (s k) -> p s k", k=2), op0=ALU.add, op1=ALU.mult))
            step(dve.tensor_tensor(ids[:, :, :], ids[:, :, :], is_pad[:, :, :], ALU.add))
            step(dve.tensor_copy(ids_i[:, :, :], ids[:, :, :]))
            dve.tensor_copy(idx_all[:, :].rearrange("p (s k) -> p s k", k=2),
                            pads1[:, 0:1, :].broadcast_to([P, S * ITEMS // 2 + TSLOTS, 2])).then_inc(idx_ready, 1)
            dve.wait_ge(meta_ready, 1)
            for e in range(E):
                before = dve.value_load(meta[0:1, 1, e:e + 1], min_val=0, max_val=ITEMS)
                dve.wait_ge(idx_ready, e + 1)
                dve.tensor_copy(idx_all[:, bass.ds(S * before, TSLOTS)], ids_i[:, e, :]).then_inc(idx_ready, 1)

            def split_input(m):
                dve.wait_ge(gathered, 32 * (m + 1))
                dve.tensor_scalar(w_sel[:, bass.ds(m + 1, 1), :, 1:].rearrange("p o k e -> p (o k) e"), h_sel[:, :, C:ROW], 0.0, None,
                                  ALU.add).then_inc(w_copied, 1)

            def split_input2(m):
                dve.wait_ge(sel_hi, m + 1)
                dve.tensor_tensor(hs_lo[:, :, :].rearrange("p k t -> p (k t)"), psM[:, 0, :],
                                  hs_hi[:, :, :].rearrange("p k t -> p (k t)").bitcast(F32), ALU.subtract).then_inc(sel_lo, 1)

            def product(m, h):
                dve.wait_ge(silu_ready, 2 * m + h + 1 + FREE)
                dve.wait_ge(up_ps, 2 * m + h + 1)
                dve.tensor_tensor(a_full[:, h, :], psS[:, 1, h, :], silu_g[:, h, :], ALU.mult).then_inc(a_ready, 1)

            def split_hidden(m, h):
                dve.wait_ge(a_ready, 2 * m + h + 1 + FREE)
                dve.wait_ge(a_rounded, 2 * m + h + 1)
                dve.tensor_tensor(a_lo[:, 2 * h:2 * h + 2, :].rearrange("p i t -> p (i t)"), a_full[:, h, :],
                                  a_hi[:, 2 * h:2 * h + 2, :].rearrange("p i t -> p (i t)").bitcast(F32),
                                  ALU.subtract).then_inc(a_split, 1)

            def output(e1, m):
                dve.wait_ge(down_ps, 2 * m + 2 + FREE)
                dve.wait_ge(scattered, ZEROING + 32 * m)
                for k in range(S):
                    dve.tensor_scalar(y_sel[:, k, :], psY[:, k, 0:C],
                                      w_sel[:, bass.ds(m + 1, 1), k, bass.ds(e1, 1)].rearrange("p a b -> p (a b)"), None,
                                      ALU.mult).then_inc(y_ready, 1)

            def body(e, e2, first, m, half):
                product(m, 0)
                split_input(m + 1)
                split_input2(m + 1)
                split_hidden(m, 0)
                product(m, 1)
                if first and half == 0:
                    with dve.If(e2 > 0):
                        output(e, m - 1)
                else:
                    output(e if first else e + 1, m - 1)
                split_hidden(m, 1)

            def between_experts(e, e2, half, before):
                if half == 0:
                    split_weights(e + 1, 1)
                else:
                    with dve.If(e2 < E // 2 - 1):
                        split_weights(e + 1, 0)

            split_input(0)
            split_input2(0)
            walk_items(dve, body, between_experts)
            items = dve.value_load(meta[0:1, 2, E - 1:E], min_val=E, max_val=ITEMS)
            output(E, items - 1)
            for t in range(NT):
                if t % TT == 0:
                    dve.wait_ge(y_in[t // TT], 16)
                dve.tensor_tensor(y_all[:, t, :], y_all[:, t, :], mod_rows[:, B + t // TT, :], ALU.mult).then_inc(out_step, 1)
                dve.wait_ge(out_step, t + 1)
                dve.tensor_tensor(y_all[:, t, :], y_all[:, t, :], x_all[:, t, :], ALU.add).then_inc(out_ready, 1)

        @block.tensor
        def _(pe):
            for freed, n in ((q_turned, 4), (k_turned, 2), (pv_done, 4), (yT2_ps, KC), (logit_ps, 3), (down_ps, FREE)):
                pe.sem_inc(freed, n)
            pe.wait_ge(wmod_in, 16)
            pe.wait_ge(silu_step, 4)
            for n, m in enumerate((SHIFT_A, SCALE_A)):
                for k in range(KC):
                    for j in range(KC):
                        mm = pe.matmul(psM[:, 0, (n * KC + k) * B:(n * KC + k + 1) * B],
                                       w_mod[:, j, m * C + k * P:m * C + (k + 1) * P], silu_c[:, j, :],
                                       start=j == 0, stop=j == KC - 1)
            mm.then_inc(modc_ps, 1)
            def turn_x(n, first):
                pe.wait_ge(xhat_done, (n + 1) * TT)
                if not first:
                    pe.wait_ge(hT2_done, n * KC)
                    pe.wait_ge(yn_done, (n - 1) * G + G - 1)
                    pe.wait_ge(trk_done, 2 * n)
                    pe.wait_ge(tr_done, n * TT)
                    pe.wait_ge(logit_done, n)
                for k in range(KC):
                    for tt in range(TT):
                        mm = pe.transpose(psM[:, k, tt * P:(tt + 1) * P], xhat[:, tt, k * P:(k + 1) * P], ident[:, :])
                    mm.then_inc(xT_ps, 1)

            def project_qkv(n, first, pair):
                if pair == 0:
                    pe.wait_ge(hT_done, (n + 1) * KC + 1)
                    if not first:
                        pe.wait_ge(yn_done, n * G)
                else:
                    pe.wait_ge(qkv_sb, n * TT + 2)
                for tt in (2 * pair, 2 * pair + 1):
                    for k in range(KC):
                        mm = pe.matmul(psM[:, tt % 2, 0:QKV], hT[:, k, tt * P:(tt + 1) * P], w_qkv[:, k, :],
                                       start=k == 0, stop=k == KC - 1)
                    mm.then_inc(qkv_ps, 1)

            def turn_q(n, first, end, tt):
                m = n * TT + tt
                pe.wait_ge(parts_done, 4 * (m + 1))
                pe.wait_ge(lo_done, 2 * (m + 1) + 1)
                if tt == 0:
                    pe.wait_ge(qkv_sb, (n + 1) * TT)
                    if end:
                        pe.wait_ge(o_gated, (n - 1) * TT)
                    elif not first:
                        pe.wait_ge(yn_done, (n - 1) * G + 1 + G)
                elif tt == 2:
                    pe.wait_ge(trk_done, 2 * n + 1)
                    pe.wait_ge(tr_done, n * TT + tt)
                    if not first:
                        pe.wait_ge(yn_done, (n - 1) * G + 2 + G)
                else:
                    pe.wait_ge(trq_done, n * TT + tt)
                    pe.wait_ge(tr_done, n * TT + tt)
                for half in range(2):
                    for j in range(H // 2):
                        mm = pe.transpose(psM_b[0:QW, half, j * P:(j + 1) * P],
                                          q6[:, tt % 2, half * H // 2 + j, :, :].rearrange("p a d -> p (a d)"), ident_b[:, :])
                    mm.then_inc(q_turned, 1)

            def turn_k(n, pair):
                pe.wait_ge(trq_done, n * TT + 2 * pair + 2)
                for tt in (2 * pair, 2 * pair + 1):
                    for j in range(G):
                        at = (2 * j + tt % 2) * P
                        mm = pe.transpose(psM_b[0:QW, 0, at:at + P], k6[:, tt, j, :, :].rearrange("p a d -> p (a d)"),
                                          ident_b[:, :])
                mm.then_inc(k_turned, 1)

            def score(b, parity, u):
                gk, pair = u // 2, u % 2
                g, kt = gk // TT, gk % TT
                if u < 2:
                    pe.wait_ge(trq_done, (b + 1) * TT)
                    pe.wait_ge(tr_done, (b + 1) * TT)
                    pe.wait_ge(trk_done, 2 * (b + 1))
                pe.wait_ge(probs_done, b * UNITS + u + 1)
                for j in range(2):
                    mm = pe.matmul(psS[:, u % 2, j, :], kT[:, parity, g, kt * P:(kt + 1) * P],
                                   qT[:, parity, g * R + 2 * pair + j, :], start=True, stop=True)
                mm.then_inc(scores, 1)

            def turn_y(b, g, begin, end):
                pe.wait_ge(y_sb, b * G + g + 1 + 2)
                if g == 0:
                    if begin:
                        pe.wait_ge(qkv_sb, (b + 2) * TT)
                    if end:
                        pe.wait_ge(yT2_done, b * KC)
                elif g == G - 1:
                    pe.wait_ge(logit_done, b + 2)
                    if begin:
                        pe.wait_ge(hT_done, (b + 3) * KC + 1)
                else:
                    if begin and g == 1:
                        pe.wait_ge(tr_done, (b + 1) * TT + 2)
                    if begin and g == 2:
                        pe.wait_ge(trk_done, 2 * (b + 1) + 2)
                    if end:
                        pe.wait_ge(o_gated, b * TT)
                for tt in range(TT):
                    mm = pe.transpose(psM[:, g % 2, tt * P:(tt + 1) * P], yT[:, g % 2, tt * P:(tt + 1) * P],
                                      ident[:, :])
                mm.then_inc(yback_ps, 1)

            def turn_outputs(p, begin):
                pe.wait_ge(y_done, (p + 1) * G)
                pe.wait_ge(hT2_done, (p + 2) * KC)
                if begin:
                    pe.wait_ge(qkv_sb, (p + 3) * TT)
                for k in range(KC):
                    for tt in range(TT):
                        mm = pe.transpose(psM[:, k, tt * P:(tt + 1) * P], y_nat[:, tt, k * P:(k + 1) * P], ident[:, :])
                    mm.then_inc(yT2_ps, 1)

            def project_outputs(p, within):
                pe.wait_ge(yT2_done, (p + 1) * KC)
                if within:
                    pe.wait_ge(yn_done, (p + 1) * G + 1 + G)
                for tt in range(TT):
                    for k in range(KC):
                        mm = pe.matmul(psM[:, tt // 2, (tt % 2) * C:(tt % 2 + 1) * C], hT[:, k, tt * P:(tt + 1) * P],
                                       w_o[:, k, :], start=k == 0, stop=k == KC - 1)
                    if tt % 2:
                        mm.then_inc(o_ps, 1)

            def turn_h(p, nth, begin, within):
                k = KC - 1 - nth
                pe.wait_ge(h_done, (p + 1) * TT)
                if nth == 0 and begin:
                    pe.wait_ge(tr_done, (p + 3) * TT)
                elif within:
                    pe.wait_ge(yn_done, (p + 1) * G + 2 + nth + G)
                for tt in range(TT):
                    mm = pe.transpose(psM[:, k, tt * P:(tt + 1) * P], h_nat[:, tt, k * P:(k + 1) * P], ident[:, :])
                mm.then_inc(h_turned, 1)

            def route(p):
                pe.wait_ge(hT2_done, (p + 3) * KC)
                for tt in range(TT):
                    for k in range(KC):
                        mm = pe.matmul(psM[:, 1, tt * E:(tt + 1) * E], hT[:, k, tt * P:(tt + 1) * P], w_r[:, k, :],
                                       start=k == 0, stop=k == KC - 1)
                mm.then_inc(logit_ps, 1)

            pe.wait_ge(consts, NCONST)
            pe.wait_ge(modc_done, 2)
            turn_x(0, True)
            pe.wait_ge(wattn_in, 80)
            project_qkv(0, True, 0)
            project_qkv(0, True, 1)
            pe.wait_ge(silu_done, 1)
            for m in range(4 * B):
                if m >= 2:
                    pe.wait_ge(row_copied, m - 1)
                at = (GATE_A, GATE_B, SHIFT_B, SCALE_B)[m // B] * C
                for j in range(KC):
                    mm = pe.matmul(psY[:, m % 2, 0:C], silu_wide[:, j, m % B, :], w_mod[:, j, at:at + C],
                                   start=j == 0, stop=j == KC - 1)
                mm.then_inc(modr_ps, 1)
            for pair in range(2):
                turn_q(0, True, False, 2 * pair)
                turn_q(0, True, False, 2 * pair + 1)
                turn_k(0, pair)
            score(0, 0, 0)
            score(0, 0, 1)
            pe.wait_ge(row_copied, 4 * B)

            def body(b, parity, begin, end):
                pe.wait_ge(v_done, 2 * (b + 1) * TT + 1)
                for gk in range(G * TT):
                    g, kt = gk // TT, gk % TT
                    if gk + 1 < G * TT:
                        score(b, parity, 2 * gk + 2)
                        score(b, parity, 2 * gk + 3)
                    elif begin:
                        score(b + 1, 1 - parity, 0)
                        score(b + 1, 1 - parity, 1)
                    if kt == 0:
                        pe.wait_ge(y_sb, b * G + g + 1)
                    pe.wait_ge(probs_done, b * UNITS + 2 * gk + 2 + 2)
                    for r in range(R):
                        mm = pe.matmul(psY[r * YROWS:(r + 1) * YROWS, g % 2, :], v_aug[:, parity, kt, g, :],
                                       probs[:, gk % 4, r, :], start=kt == 0, stop=kt == TT - 1)
                    mm.then_inc(pv_done, 1)
                    if begin:
                        if gk == 0:
                            turn_x(b + 1, False)
                        elif gk in (2, 3):
                            project_qkv(b + 1, False, gk - 2)
                        elif gk in (7, 8, 10, 11):
                            turn_q(b + 1, False, end, {7: 0, 8: 1, 10: 2, 11: 3}[gk])
                        elif gk in (9, 12):
                            turn_k(b + 1, (gk - 9) // 3)
                    if gk in (5, 9, 13):
                        turn_y(b, (gk - 5) // 4, begin, end)
                    if end:
                        if gk == 1:
                            turn_y(b - 1, G - 1, begin, end)
                        elif gk == 4:
                            turn_outputs(b - 1, begin)
                        elif gk == 6:
                            project_outputs(b - 1, True)
                        elif gk in (12, 14):
                            turn_h(b - 1, (gk - 12) // 2, begin, True)
                        elif gk == 15:
                            route(b - 1)

            attention(pe, body)
            turn_y(B - 1, G - 1, False, True)
            turn_outputs(B - 1, False)
            project_outputs(B - 1, False)
            turn_h(B - 1, 0, False, False)
            turn_h(B - 1, 1, False, False)
            route(B - 1)

            pe.wait_ge(rt_kept, 2)
            kept = keep_b[:, :, :].rearrange("p t e -> p (t e)")
            pe.matmul(psM[:, 0, 0:NT * E], earlier[:, :], kept, start=True, stop=True)
            pe.matmul(psM[:, 1, 0:NT * E], ones_b[:, :], kept, start=True, stop=True).then_inc(rank_ps, 1)
            pe.wait_ge(y_sb, B * G + 2)
            pe.wait_ge(probs_done, B * UNITS + 2)
            for e in range(E):
                pe.wait_ge(one_done, e + 1)
                for tt in range(NT):
                    mm = pe.matmul(psY[:, 0, e * 2 * TSLOTS:(e + 1) * 2 * TSLOTS], one_row[:, e % 2, tt, :],
                                   values[:, tt, e, :, :].rearrange("p v s -> p (v s)"), start=tt == 0, stop=tt == NT - 1)
                mm.then_inc(lists_ps, 1)

            def turn(m):
                pe.wait_ge(gathered, 32 * (m + 1))
                for k in range(KC):
                    for j in range(S):
                        mm = pe.transpose(psM[:, 0, k * SW + j * P:k * SW + (j + 1) * P], h_sel[:, j, k * P:(k + 1) * P],
                                          ident[:, :])
                mm.then_inc(turned, 1)

            def gate_up(m, half, h):
                for part, (ps, ready, used) in enumerate(((psS[:, 0, h, :], gate_ps, silu_ready),
                                                          (psS[:, 1, h, :], up_ps, a_ready))):
                    pe.wait_ge(used, 2 * m + h - 1 + FREE)
                    for i in range(2):
                        at = 0
                        for k in range(KC):
                            cols = slice(k * I + (2 * h + i) * P, k * I + (2 * h + i + 1) * P)
                            hi, lo = w_hi[half][part][:, cols], w_lo[half][part][:, cols]
                            for w, v in ((hi, hs_hi), (hi, hs_lo), (lo, hs_hi)):
                                mm = pe.matmul(ps[:, i * SW:(i + 1) * SW], w, v[:, k, :], start=at == 0, stop=at == 3 * KC - 1)
                                at += 1
                    mm.then_inc(ready, 1)

            def down(m, half, h):
                pe.wait_ge(a_split, 2 * m + h + 1 + FREE)
                if h == 0:
                    pe.wait_ge(y_ready, 2 * m + FREE)
                for j in range(S):
                    tok = slice(j * P, (j + 1) * P)
                    for i in (2 * h, 2 * h + 1):
                        hi, lo = (w[half][2][:, i * C:(i + 1) * C] for w in (w_hi, w_lo))
                        for n, (v, w) in enumerate(((a_hi, hi), (a_hi, lo), (a_lo, hi))):
                            mm = pe.matmul(psY[:, j, 0:C], v[:, i, tok], w, start=i == 0 and n == 0, stop=i == KI - 1 and n == 2)
                mm.then_inc(down_ps, 1)

            def downs(m, half):
                down(m, half, 0)
                down(m, half, 1)

            def body(e, e2, first, m, half):
                if first:
                    pe.wait_ge(w_ready, 3 * e + 3)
                pe.wait_ge(sel_lo, m + 1)
                gate_up(m, half, 0)
                turn(m + 1)
                gate_up(m, half, 1)
                if first and half == 0:
                    with pe.If(e2 > 0):
                        downs(m - 1, 1)
                else:
                    downs(m - 1, 1 - half if first else half)

            pe.wait_ge(meta_ready, 1)
            turn(0)
            walk_items(pe, body, lambda *a: None)
            items = pe.value_load(meta[0:1, 2, E - 1:E], min_val=E, max_val=ITEMS)
            downs(items - 1, 1)


_INS = ["x", "wqT", "wkT", "wvT", "woT", "routerT", "gateT", "upT", "downT", "cT", "wmod"]


def kernel(L0_attn_x, L0_attn_Wq, L0_attn_Wk, L0_attn_Wv, L0_attn_Wo, L0_ffn_router_w, L0_ffn_gate_w, L0_ffn_up_w,
           L0_ffn_down_w, L0_c, L0_wmod):
    import concourse.bacc as bacc
    import numpy as np
    from concourse.bass_utils import run_bass_kernel_spmd

    turned = [np.swapaxes(w, -1, -2) for w in (L0_attn_Wq, L0_attn_Wk, L0_attn_Wv, L0_attn_Wo, L0_ffn_router_w,
                                               L0_ffn_gate_w, L0_ffn_up_w, L0_ffn_down_w, L0_c)]
    arrays = dict(zip(_INS, map(np.ascontiguousarray, [L0_attn_x, *turned, L0_wmod])))
    nc = bacc.Bacc("TRN2", target_bir_lowering=False, num_devices=1)
    args = [nc.dram_tensor(k, v.shape, mybir.dt.from_np(v.dtype), kind="ExternalInput").ap() for k, v in arrays.items()]
    out = nc.dram_tensor("out", arrays["x"].shape, mybir.dt.from_np(arrays["x"].dtype), kind="ExternalOutput").ap()
    adaln_block(nc, *args, out)
    return run_bass_kernel_spmd(nc, [arrays], core_ids=[0]).results[0]["out"]
```

```python
from contextlib import ExitStack

import concourse.bass as bass
import concourse.mybir as mybir

F32 = mybir.dt.float32
F32R = mybir.dt.float32r
BF16 = mybir.dt.bfloat16
F16 = mybir.dt.float16
I32 = mybir.dt.int32
ALU = mybir.AluOpType
ACT = mybir.ActivationFunctionType
AX = mybir.AxisListType

P = 128
LN_EPS = 1e-5
RMS_EPS = 1.1920928955078125e-07
L2_EPS_SQUARED = 1e-24
TOP_P = 0.9
GATE_LEAST = 0.25
SHIFT_A, SCALE_A, GATE_A, SHIFT_B, SCALE_B, GATE_B = range(6)


def adaln_block(nc, x, wqT, wkT, wvT, woT, routerT, gateT, upT, downT, cT, wmod, out):
    B, N, C = x.shape
    KC = C // P
    TT = N // P
    NT = B * TT
    T = B * N
    KV = wkT.shape[1]
    QKV = C + 2 * KV
    D = 16
    H = C // D
    G = KV // D
    R = H // G
    HG = H + G
    ALLH = H + 2 * G
    E, _, I = gateT.shape
    KI = I // P
    TERMS = 6
    QW = TERMS * D
    ATT_SCALE = float(D) ** -0.5
    UNITS = G * TT * 2
    YROWS = 32
    S = 2
    TSLOTS = T // P
    ITEMS = E * TSLOTS // S
    ROW = C + E
    PADS = S * P
    SW = S * P
    GATE_ROW, SHIFT_ROW, SCALE_ROW = 0, 2 * B, 3 * B

    ctx = ExitStack()
    with ctx:
        attention_only = ctx.enter_context(ExitStack())
        h_rows = nc.dram_tensor("h_rows", [T + PADS, ROW], F32)
        mod_table = nc.dram_tensor("mod_table", [B, 4 * C], F32)
        y_rows = nc.dram_tensor("y_rows", [T + PADS, C], F32)

        def sb(name, shape, dt=F32):
            return ctx.enter_context(nc.sbuf_tensor(name, shape, dt))

        def att(name, shape, dt=F32):
            return attention_only.enter_context(nc.sbuf_tensor(name, shape, dt))

        def sem(name):
            return ctx.enter_context(nc.semaphore(name))

        def sems(names):
            return [sem(n) for n in names.split()]

        x_all = sb("x_all", [P, NT, C])
        logits = sb("logits", [P, NT, E])
        moe_w = sb("moe_w", [P, NT, E])
        mod_rows = sb("mod_rows", [P, 4 * B, C])
        ident = sb("ident", [P, P])
        ident_b = sb("ident_b", [P, P], BF16)
        minus_half = sb("minus_half", [P, NT])
        zeros = sb("zeros", [P, ROW])
        idle = sb("idle", [P, 1])
        tie = sb("tie", [P, E, E])
        earlier = sb("earlier", [P, P], BF16)
        ones_b = sb("ones_b", [P, P], BF16)
        slot_row = sb("slot_row", [P, P, NT], F16)
        slot_tile = sb("slot_tile", [P, TSLOTS, NT, E], F16)
        token1 = sb("token1", [P, NT, E], F16)
        pad_row = sb("pad_row", [P, E, TSLOTS // 2, 2])
        rt_max = sb("rt_max", [P, NT])
        rt_sum = sb("rt_sum", [P, NT])
        rt_p = sb("rt_p", [P, NT, E])
        rt_before = sb("rt_before", [P, NT, E])
        keep = sb("keep", [P, NT, E])
        keep_b = sb("keep_b", [P, NT, E], BF16)
        w_in = [sb(f"w_in{n}", [P, I * KC]) for n in range(3)]
        setup_only = ctx.enter_context(ExitStack())
        w_mod = setup_only.enter_context(nc.sbuf_tensor("w_mod", [P, KC, 6 * C], F32))
        mod_small = setup_only.enter_context(nc.sbuf_tensor("mod_small", [P, 4 * C], F32))
        setup_only.close()
        w_hi, w_lo = ([[sb(f"{part}0_{n}", [P, I * KC], F32R) for n in range(3)]] for part in ("w_hi", "w_lo"))

        w_qkv = att("w_qkv", [P, KC, QKV])
        w_o = att("w_o", [P, KC, C])
        w_r = att("w_r", [P, KC, E])
        mod_cols = att("mod_cols", [P, 2, KC, B])
        silu_c = att("silu_c", [P, KC, B])
        silu_t = att("silu_t", [P, KC, B])
        stats1 = att("stats1", [P, NT, 6])
        mean_var1 = att("mean_var1", [P, NT, 2])
        var_eps1 = att("var_eps1", [P, NT])
        rstd1 = att("rstd1", [P, NT])
        stats = att("stats", [P, TT, 6])
        mean_var = att("mean_var", [P, TT, 2])
        var_eps = att("var_eps", [P, TT])
        rstd = att("rstd", [P, TT])
        idle_v = att("idle_v", [P, 1])
        xhat = att("xhat", [P, TT, C])
        h_nat = att("h_nat", [P, TT, C])
        hT = att("hT", [P, KC, N])
        mods = att("mods", [P, 2, KC])
        qkv = att("qkv", [P, TT, QKV])
        squares = att("squares", [P, QKV])
        norms = att("norms", [P, TT, ALLH])
        rnorm = att("rnorm", [P, TT, ALLH])
        newton = att("newton", [P, TT * ALLH])
        q6 = att("q6", [P, 2, H, TERMS, D], BF16)
        k6 = att("k6", [P, TT, G, TERMS, D], BF16)
        vn = att("vn", [P, 2, TT, G, D])
        v_aug = att("v_aug", [P, 2, TT, G, YROWS])
        qT = att("qT", [QW, 2, H, N], BF16)
        kT = att("kT", [QW, 2, G, N], BF16)
        probs = att("probs", [P, 4, R, N])
        yT = att("yT", [P, 2, N])
        rden = att("rden", [P, TT, R])
        yn = att("yn", [P, TT, R, D])
        prod = att("prod", [P, TT, R, D])
        dots = att("dots", [P, TT, R])
        y_nat = att("y_nat", [P, TT, C])
        attention_only.close()

        for parts, part in ((w_hi, "w_hi"), (w_lo, "w_lo")):
            parts.append([sb(f"{part}1_{n}", [P, I * KC], F32R) for n in range(3)])
        rank = sb("rank", [P, NT, E])
        run = [sb(f"run{n}", [P, NT, E]) for n in range(2)]
        rank_i = sb("rank_i", [P, NT, E], I32)
        tile_i = sb("tile_i", [P, NT, E], I32)
        row_i = sb("row_i", [P, NT, E], I32)
        row_f = sb("row_f", [P, NT, E])
        tile_h = sb("tile_h", [P, NT, E], F16)
        row_h = sb("row_h", [P, E, NT], F16)
        one_tile = sb("one_tile", [P, TSLOTS, NT, E], F16)
        one_row = sb("one_row", [P, 2, P, NT], F16)
        is_pad = sb("is_pad", [P, E, TSLOTS])
        ids_i = sb("ids_i", [P, E, TSLOTS], I32)
        idx_all = sb("idx_all", [P, S * ITEMS + 2 * TSLOTS], I32)
        cnt_i = sb("cnt_i", [P, E], I32)
        cnt_f = [sb(f"cnt_f{n}", [P, E]) for n in range(2)]
        items_f = sb("items_f", [P, E])
        meta = sb("meta", [P, 3, E], I32)
        idx_in = sb("idx_in", [P, S], I32)
        idx_out = sb("idx_out", [P, S], I32)
        h_sel = sb("h_sel", [P, S, ROW])
        hs_hi = sb("hs_hi", [P, KC, SW], F32R)
        hs_lo = sb("hs_lo", [P, KC, SW], F32R)
        w_sel = sb("w_sel", [P, ITEMS + TSLOTS, S, E + 1])
        silu_g = sb("silu_g", [P, 2, 2 * SW])
        a_full = sb("a_full", [P, 2, 2 * SW])
        a_hi = sb("a_hi", [P, KI, SW], F32R)
        a_lo = sb("a_lo", [P, KI, SW], F32R)
        y_sel = sb("y_sel", [P, S, C])
        y_all = sb("y_all", [P, NT, C])

        psS = ctx.enter_context(nc.psum_tensor("psS", [P, 2, 2, 512], F32))
        psY = ctx.enter_context(nc.psum_tensor("psY", [P, 2, 512], F32))
        psM = ctx.enter_context(nc.psum_tensor("psM", [P, 2, 512], F32))
        psM_b = psM[:, :, :].bitcast(BF16)

        c_in, wmod_in, wmod_rest_in, wattn_in, wrest_in, x0_in, x_in, y_out = sems(
            "c_in wmod_in wmod_rest_in wattn_in wrest_in x0_in x_in y_out")
        w_loaded = [sem(f"w_loaded{n}") for n in range(3)]
        y_in = [sem(f"y_in{b}") for b in range(B)]
        (zeroed, ident_done, consts, silu_step, modc_ps, modc_done, modr_ps, row_copied, mod_out, mod_in, gate_step,
         modr_done, idle_done) = sems(
            "zeroed ident_done consts silu_step modc_ps modc_done modr_ps row_copied mod_out mod_in gate_step "
            "modr_done idle_done")
        (bn1_done, ln1_stats, ln1_eps, ln1_rstd, mods_done, xhat_done, xT_ps, hT_done, qkv_ps, qkv_sb, squared, sq_sum,
         newton_step, v_done, hi_done, rest_done, mid_done, lo_done, parts_done, q_turned, k_turned, trq_done, tr_done,
         trk_done) = sems(
            "bn1_done ln1_stats ln1_eps ln1_rstd mods_done xhat_done xT_ps hT_done qkv_ps qkv_sb squared sq_sum "
            "newton_step v_done hi_done rest_done mid_done lo_done parts_done q_turned k_turned trq_done tr_done "
            "trk_done")
        (scores, probs_done, pv_done, y_sb, yback_ps, rden_done, yn_done, prod_done, dots_done, along_done, y_done) = sems(
            "scores probs_done pv_done y_sb yback_ps rden_done yn_done prod_done dots_done along_done y_done")
        (yT2_ps, yT2_done, o_ps, o_gated, x2_done, idle_v_done, bn_done, ln_stats, ln_eps, ln_rstd, xhat2_done, h_scaled,
         h_done, h_out, h_turned, hT2_done, logit_ps, logit_done) = sems(
            "yT2_ps yT2_done o_ps o_gated x2_done idle_v_done bn_done ln_stats ln_eps ln_rstd xhat2_done h_scaled "
            "h_done h_out h_turned hT2_done logit_ps logit_done")
        rt_step, rt_exp, rt_kept, w_out, rank_ps, one_done, lists_ps, idx_ready, meta_ready = sems(
            "rt_step rt_exp rt_kept w_out rank_ps one_done lists_ps idx_ready meta_ready")
        (w_rounded, w_ready, gate_ps, up_ps, silu_ready, a_ready, a_rounded, a_split, down_ps, turned, sel_hi, sel_lo,
         w_copied, idx_copied, gathered, scattered, y_ready, out_step, out_ready) = sems(
            "w_rounded w_ready gate_ps up_ps silu_ready a_ready a_rounded a_split down_ps turned sel_hi sel_lo "
            "w_copied idx_copied gathered scattered y_ready out_step out_ready")
        block = ctx.enter_context(nc.Block())

        w_src = [w.rearrange("e (k p) n -> e p k n", p=P) for w in (gateT, upT, downT)]
        ROUTE_STEPS = 12
        NCONST = 8
        FREE = 2
        SETTLED = 4

        def attention(eng, body):
            body(0, 0, True, False)
            with eng.Fori(0, (B - 2) // 2) as pair:
                body(2 * pair + 1, 1, True, True)
                body(2 * pair + 2, 0, True, True)
            body(B - 1, 1, False, True)

        def settle(pool, before):
            pool.wait_ge(idle_done, before + SETTLED)
            pool.tensor_tensor(idle[:, :], minus_half[:, 0:1], minus_half[:, 0:1], ALU.mult).then_inc(idle_done, 1)

        def settle_v(dve, before):
            dve.wait_ge(idle_v_done, before + 1)
            dve.memset(idle_v[:, :], 0.0).then_inc(idle_v_done, 1)

        def item_counts(eng, e):
            n = eng.value_load(meta[0:1, 0, bass.ds(e, 1)], min_val=1, max_val=TSLOTS // S)
            before = eng.value_load(meta[0:1, 1, bass.ds(e, 1)], min_val=0, max_val=ITEMS)
            return n, before

        def walk_items(eng, body, between):
            with eng.Fori(0, E // 2) as e2:
                for half in range(2):
                    e = 2 * e2 + half
                    n, before = item_counts(eng, e)
                    body(e, e2, True, before, half)
                    between(e, e2, half, before)
                    for i in range(1, 3):
                        with eng.If(n > i):
                            body(e, e2, False, before + i, half)
                    with eng.If(n > 3):
                        with eng.Fori(3, TSLOTS // S) as i:
                            with eng.If(n > i):
                                body(e, e2, False, before + i, half)

        ZEROING = 64

        @block.sync
        def _(sp):
            sp.sem_inc(h_out, 16)
            sp.dma_start(silu_c[:, :, :], cT.rearrange("(k p) b -> p k b", p=P)).then_inc(c_in, 16)
            sp.dma_start(x_all[:, 0:TT, :], x[0].rearrange("(t p) c -> p t c", p=P)).then_inc(x0_in, 16)
            sp.dma_start(w_mod[:, :, 0:2 * C], wmod[:, 0:2 * C].rearrange("(k p) n -> p k n", p=P)).then_inc(wmod_in, 16)
            for w, (a, z) in ((wqT, (0, C)), (wkT, (C, C + KV)), (wvT, (C + KV, QKV))):
                sp.dma_start(w_qkv[:, :, a:z], w.rearrange("(k p) n -> p k n", p=P)).then_inc(wattn_in, 16)
            sp.dma_start(w_mod[:, :, 2 * C:], wmod[:, 2 * C:].rearrange("(k p) n -> p k n", p=P)).then_inc(wmod_rest_in, 16)
            sp.dma_start(w_o[:, :, :], woT.rearrange("(k p) n -> p k n", p=P)).then_inc(wrest_in, 16)
            sp.dma_start(w_r[:, :, :], routerT.rearrange("(k p) n -> p k n", p=P)).then_inc(wrest_in, 16)
            for b in range(1, B):
                sp.dma_start(x_all[:, b * TT:(b + 1) * TT, :],
                             x[b].rearrange("(t p) c -> p t c", p=P)).then_inc(x_in, 16)
            def load_weights(e, apart=False):
                for n in range(3):
                    if n and apart:
                        sp.wait_ge(w_loaded[n - 1], 16 * (e + 1))
                    sp.dma_start(w_in[n][:, :].rearrange("p (k n) -> p k n", k=w_src[n].shape[2]),
                                 w_src[n][e]).then_inc(w_loaded[n], 16)

            load_weights(0)
            sp.wait_ge(row_copied, 2)
            sp.dma_start(mod_table[:, :], mod_small[0:B, :]).then_inc(mod_out, 16)
            sp.wait_ge(mod_out, 16)
            for n, m in enumerate((GATE_A, GATE_B, SHIFT_B, SCALE_B)):
                a = (m - GATE_A) * C
                sp.dma_start(mod_rows[:, n * B:(n + 1) * B, :], mod_table[:, a:a + C].rearrange(
                    "(o b) c -> o b c", o=1).broadcast_to([P, B, C])).then_inc(mod_in, 16)
            with sp.Fori(0, B) as b:
                sp.wait_ge(h_done, (b + 1) * TT)
                sp.dma_start(h_rows[bass.ds(b * N, N), 0:C].rearrange("(t p) c -> p t c", p=P),
                             h_nat[:, :, :]).then_inc(h_out, 16)
            sp.wait_ge(rt_kept, 4)
            sp.dma_start(h_rows[0:T, C:ROW].rearrange("(t p) e -> p t e", p=P), moe_w[:, :, :]).then_inc(w_out, 16)
            with sp.Fori(1, E) as e:
                sp.wait_ge(w_ready, e * 3)
                load_weights(e, apart=True)
            sp.wait_ge(meta_ready, 1)
            items = sp.value_load(meta[0:1, 2, E - 1:E], min_val=E, max_val=ITEMS)
            sp.wait_ge(modr_done, 3)
            sp.wait_ge(scattered, ZEROING + 32 * items)
            for b in range(B):
                sp.dma_start(y_all[:, b * TT:(b + 1) * TT, :],
                             y_rows[b * N:(b + 1) * N, :].rearrange("(t p) c -> p t c", p=P)).then_inc(y_in[b], 16)
            for b in range(B):
                sp.wait_ge(out_ready, b + 1)
                sp.dma_start(out[b].rearrange("(t p) c -> p t c", p=P), y_all[:, b * TT:(b + 1) * TT, :]).then_inc(y_out, 16)
            sp.wait_ge(y_out, 16 * B)

        @block.gpsimd
        def _(pool):
            pool.sem_inc(idle_done, SETTLED)
            pool.memset(minus_half[:, :], -0.5).then_inc(zeroed, 1)
            for m in (ident, ident_b):
                pool.memset(m[:, :], 0.0).then_inc(zeroed, 1)
            pool.wait_ge(zeroed, 3)
            for m in (ident, ident_b):
                pool.affine_select(out=m[:, :], in_=m[:, :], compare_op=ALU.not_equal, fill=1.0, base=0,
                                   pattern=[[-1, P]], channel_multiplier=1).then_inc(ident_done, 1)
            pool.wait_ge(ln1_eps, 1)
            pool.tensor_tensor(rstd1[:, 0:TT], var_eps1[:, 0:TT], minus_half[:, 0:TT], ALU.pow).then_inc(ln1_rstd, 1)
            for m, v in ((v_aug[:, :, :, :, D:YROWS], 0.0), (tie[:, :, :], 1.0), (earlier[:, :], 1.0), (zeros[:, :], 0.0)):
                pool.memset(m, v).then_inc(zeroed, 1)
            pool.wait_ge(zeroed, 7)
            pool.affine_select(out=tie[:, :, :], in_=tie[:, :, :], compare_op=ALU.is_gt, fill=0.0, base=0,
                               pattern=[[1, E], [-1, E]], channel_multiplier=0).then_inc(consts, 1)
            pool.affine_select(out=earlier[:, :], in_=earlier[:, :], compare_op=ALU.is_gt, fill=0.0, base=0,
                               pattern=[[1, P]], channel_multiplier=-1).then_inc(consts, 1)
            pool.memset(ones_b[:, :], 1.0).then_inc(consts, 1)
            pool.memset(v_aug[:, :, :, :, D:D + 1], 1.0).then_inc(consts, 1)
            small = dict(allow_small_or_imprecise_dtypes=True)
            pool.iota(slot_row[:, :, :], [[1, P], [0, NT]], base=0, channel_multiplier=0, **small).then_inc(consts, 1)
            pool.iota(slot_tile[:, :, :, :], [[1, TSLOTS], [0, NT], [0, E]], base=0, channel_multiplier=0,
                      **small).then_inc(consts, 1)
            pool.iota(token1[:, :, :], [[P, NT], [0, E]], base=1, channel_multiplier=1, **small).then_inc(consts, 1)
            pool.iota(pad_row[:, :, :, :], [[0, E], [0, TSLOTS // 2], [P, 2]], base=T + 1, channel_multiplier=1,
                      **small).then_inc(consts, 1)
            pool.wait_ge(consts, NCONST)
            pool.wait_ge(ln1_eps, 2)
            pool.tensor_tensor(rstd1[:, TT:], var_eps1[:, TT:], minus_half[:, 0:NT - TT], ALU.pow).then_inc(ln1_rstd, 1)
            for r0, r1 in ((0, T // 2), (T // 2, T), (T, T + PADS)):
                pool.dma_start(y_rows[r0:r1, :].rearrange("(t p) c -> p t c", p=P),
                               zeros[:, 0:C].rearrange("p (o c) -> p o c", o=1).broadcast_to([P, (r1 - r0) // P, C])
                               ).then_inc(scattered, 16)
            pool.dma_start(h_rows[T:T + PADS, :].rearrange("(t p) c -> p t c", p=P),
                           zeros[:, :].rearrange("p (o c) -> p o c", o=1).broadcast_to([P, S, ROW])).then_inc(scattered, 16)

            with pool.Fori(0, B) as b:
                pool.wait_ge(ln_eps, b + 1)
                pool.tensor_tensor(rstd[:, :], var_eps[:, :], minus_half[:, 0:TT], ALU.pow).then_inc(ln_rstd, 1)

            pool.wait_ge(h_out, 16 * (B + 1))
            pool.wait_ge(w_out, 16)
            pool.wait_ge(scattered, ZEROING)
            pool.wait_ge(idx_ready, 2)

            def gather(m, copied, settled):
                pool.tensor_copy(idx_in[:, :], idx_all[:, bass.ds(S * m, S)]).then_inc(idx_copied, 1)
                pool.wait_ge(idx_copied, copied)
                settle(pool, settled)
                for k in range(S):
                    pool.indirect_dma_start(h_sel[:, k, :], None, h_rows[:, :],
                                            bass.IndirectOffsetOnAxis(ap=idx_in[:, k:k + 1], axis=0)).then_inc(gathered, 16)

            def finish_input(m, settled):
                pool.wait_ge(turned, m + 1)
                pool.wait_ge(gathered, 32 * (m + 1))
                settle(pool, settled)
                pool.tensor_copy(w_sel[:, bass.ds(m + 1, 1), :, 1:].rearrange("p o k e -> p (o k) e"),
                                 h_sel[:, :, C:ROW]).then_inc(w_copied, 1)
                pool.wait_ge(w_copied, m + 1)

            def scatter(m, copied, settled):
                pool.wait_ge(y_ready, 2 * m + 2 + FREE)
                pool.wait_ge(scattered, ZEROING + 32 * m)
                settle(pool, settled)
                pool.tensor_copy(idx_out[:, :], idx_all[:, bass.ds(S * m, S)]).then_inc(idx_copied, 1)
                pool.wait_ge(idx_copied, copied)
                settle(pool, settled + 1)
                for k in range(S):
                    pool.indirect_dma_start(y_rows[:, :], bass.IndirectOffsetOnAxis(ap=idx_out[:, k:k + 1], axis=0),
                                            y_sel[:, k, :], None, compute_op=ALU.add).then_inc(scattered, 16)

            gather(0, 1, 0)
            pool.wait_ge(idx_ready, E + 1)
            pool.wait_ge(meta_ready, 1)
            for m in range(2):
                finish_input(m, 2 * m + 1)
                gather(m + 1, m + 2, 2 * m + 2)
            items = pool.value_load(meta[0:1, 2, E - 1:E], min_val=E, max_val=ITEMS)
            with pool.Fori(0, ITEMS // 8) as some:
                with pool.If(items > 8 * some + 2):
                    with pool.Fori(2, 10) as nth:
                        m = 8 * some + nth
                        with pool.If(items > m):
                            finish_input(m, SETTLED * m - 3)
                            gather(m + 1, 2 * m, SETTLED * m - 2)
                            scatter(m - 2, 2 * m + 1, SETTLED * m - 1)
            scatter(items - 2, 2 * items, SETTLED * items - 3)
            scatter(items - 1, 2 * items + 1, SETTLED * items - 1)

        @block.scalar
        def _(act):
            for freed, n in ((hT_done, 1), (hT2_done, 2 * KC), (probs_done, 2), (silu_ready, FREE)):
                act.sem_inc(freed, n)
            act.wait_ge(c_in, 16)
            act.activation(silu_t[:, :, :], silu_c[:, :, :], ACT.Exp, scale=-1.0).then_inc(silu_step, 1)

            def round_weights(e, half):
                for n in range(3):
                    act.wait_ge(w_loaded[n], e * 16 + 16)
                    act.copy(w_hi[half][n][:, :], w_in[n][:, :]).then_inc(w_rounded, 1)

            def scale_x(n):
                act.wait_ge(logit_ps, n + 1)
                act.wait_ge(mods_done, n + 1)
                for k in range(KC):
                    act.wait_ge(xT_ps, n * KC + k + 1)
                    act.activation(hT[:, k, :], psM[:, k, :], ACT.Identity, bias=mods[:, 0, k:k + 1],
                                   scale=mods[:, 1, k:k + 1]).then_inc(hT_done, 1)

            def take_qkv(n, tiles):
                for tt in tiles:
                    act.wait_ge(qkv_ps, n * TT + tt + 1)
                    if tt == 0:
                        act.wait_ge(lo_done, 2 * n * TT + 1)
                        act.wait_ge(v_done, 2 * n * TT + 1)
                    act.copy(qkv[:, tt, :], psM[:, tt % 2, 0:QKV]).then_inc(qkv_sb, 1)

            def repeat_parts(n, tt):
                act.wait_ge(hi_done, n * TT + tt + 1)
                act.wait_ge(mid_done, 2 * (n * TT + tt) + 2)
                q, k = q6[:, tt % 2, :, :, :], k6[:, tt, :, :, :]
                act.copy(q[:, :, 2:5:2, :], q[:, :, 0:1, :].broadcast_to([P, H, 2, D])).then_inc(parts_done, 1)
                act.copy(q[:, :, 3, :], q[:, :, 1, :]).then_inc(parts_done, 1)
                act.copy(k[:, :, 3:6:2, :], k[:, :, 0:1, :].broadcast_to([P, G, 2, D])).then_inc(parts_done, 1)
                act.copy(k[:, :, 2, :], k[:, :, 1, :]).then_inc(parts_done, 1)

            def take_q(n, parity, tt):
                act.wait_ge(q_turned, 2 * (n * TT + tt) + 2 + 4)
                act.copy(qT[:, parity, 8:16, tt * P:(tt + 1) * P],
                         psM_b[0:QW, 1, :].rearrange("p (h t) -> p h t", h=8)).then_inc(tr_done, 1)

            def take_y(p):
                act.wait_ge(logit_ps, p + 3)
                for k in range(KC):
                    act.wait_ge(yT2_ps, p * KC + k + 1 + KC)
                    act.copy(hT[:, k, :], psM[:, k, :]).then_inc(yT2_done, 1)

            def take_h(p, nth):
                k = KC - 1 - nth
                act.wait_ge(h_turned, p * KC + nth + 1)
                act.copy(hT[:, k, :], psM[:, k, :]).then_inc(hT2_done, 1)

            scale_x(0)
            take_qkv(0, range(TT))
            for j in range(2):
                act.wait_ge(modr_ps, j + 1)
                act.copy(mod_small[0:B, 2 * C * j:2 * C * (j + 1)], psY[0:B, j, 0:2 * C]).then_inc(row_copied, 1)
            for tiles in ((0, 1), (2, 3)):
                for tt in tiles:
                    repeat_parts(0, tt)
                for tt in tiles:
                    take_q(0, 0, tt)

            def body(b, parity, begin, end):
                for gk in range(G * TT):
                    for pair in range(2):
                        act.wait_ge(scores, b * UNITS + 2 * gk + pair + 1)
                        if pair == 0:
                            act.wait_ge(pv_done, b * TT * G + gk + 1)
                        act.activation(probs[:, gk % 4, 2 * pair:2 * pair + 2, :], psS[:, pair, :, :], ACT.Exp,
                                       scale=ATT_SCALE).then_inc(probs_done, 1)
                    if begin:
                        if gk == 1:
                            scale_x(b + 1)
                        elif gk == 3:
                            take_qkv(b + 1, (0, 1))
                        elif gk == 4:
                            take_qkv(b + 1, (2, 3))
                        elif gk in (6, 7, 9, 10):
                            repeat_parts(b + 1, {6: 0, 7: 1, 9: 2, 10: 3}[gk])
                        if gk in (8, 9, 11, 12):
                            take_q(b + 1, 1 - parity, {8: 0, 9: 1, 11: 2, 12: 3}[gk])
                    if end:
                        if gk == 5:
                            take_y(b - 1)
                        elif gk == 13:
                            take_h(b - 1, 0)
                        elif gk == 15:
                            take_h(b - 1, 1)
                    if not begin and gk == 8:
                        round_weights(0, 0)

            def exp_of_logits(n):
                a, z = ((0, NT - TT), (NT - TT, NT))[n]
                act.wait_ge(rt_step, ROUTE_STEPS * n + 2)
                act.activation(rt_p[:, a:z, :], rt_p[:, a:z, :], ACT.Exp).then_inc(rt_exp, 1)

            attention(act, body)
            exp_of_logits(0)
            take_y(B - 1)
            take_h(B - 1, 0)
            take_h(B - 1, 1)

            exp_of_logits(1)

            def round_input(m):
                act.wait_ge(turned, m + 1)
                act.copy(hs_hi[:, :, :].rearrange("p k t -> p (k t)"), psM[:, 0, :]).then_inc(sel_hi, 1)

            def gate(m, h):
                act.wait_ge(gate_ps, 2 * m + h + 1)
                act.wait_ge(a_ready, 2 * m + h - 1 + FREE)
                act.activation(silu_g[:, h, :], psS[:, 0, h, :], ACT.Silu).then_inc(silu_ready, 1)

            def round_hidden(m, h):
                act.wait_ge(a_ready, 2 * m + h + 1 + FREE)
                act.wait_ge(down_ps, 2 * m + h - 1 + FREE)
                act.copy(a_hi[:, 2 * h:2 * h + 2, :].rearrange("p i t -> p (i t)"), a_full[:, h, :]).then_inc(a_rounded, 1)

            def body(e, e2, first, m, half):
                gate(m, 0)
                act.wait_ge(up_ps, 2 * m + 2)
                round_input(m + 1)
                round_hidden(m, 0)
                gate(m, 1)
                round_hidden(m, 1)

            def between_experts(e, e2, half, before):
                if half == 0:
                    act.wait_ge(down_ps, 2 * before + FREE)
                    round_weights(e + 1, 1)
                else:
                    with act.If(e2 < E // 2 - 1):
                        act.wait_ge(down_ps, 2 * before + FREE)
                        round_weights(e + 1, 0)

            act.wait_ge(meta_ready, 1)
            round_input(0)
            walk_items(act, body, between_experts)

        @block.vector
        def _(dve):
            for freed, n in ((v_done, 1), (lo_done, 1), (y_sb, 2), (yn_done, G), (idle_v_done, 1), (logit_done, 2), (a_ready, FREE),
                             (a_split, FREE), (y_ready, FREE)):
                dve.sem_inc(freed, n)
            dve.wait_ge(silu_step, 1)
            dve.tensor_scalar(silu_t[:, :, :], silu_t[:, :, :], 1.0, None, ALU.add).then_inc(silu_step, 1)
            dve.wait_ge(silu_step, 2)
            dve.reciprocal(silu_t[:, :, :], silu_t[:, :, :]).then_inc(silu_step, 1)
            dve.wait_ge(silu_step, 3)
            dve.tensor_tensor(silu_c[:, :, :], silu_c[:, :, :], silu_t[:, :, :], ALU.mult).then_inc(silu_step, 1)
            def split_weights(e, half):
                for n in range(3):
                    dve.wait_ge(w_rounded, e * 3 + n + 1)
                    dve.tensor_tensor(w_lo[half][n][:, :], w_in[n][:, :], w_hi[half][n][:, :].bitcast(F32),
                                      ALU.subtract).then_inc(w_ready, 1)

            def x_tile(b, tt):
                return x_all[:, bass.ds(b * TT + tt, 1), :].rearrange("p o c -> p (o c)")

            def mean_and_variance(tiles):
                for t in tiles:
                    dve.bn_stats(stats1[:, t, :], x_all[:, t, :]).then_inc(bn1_done, 1)
                for t in tiles:
                    dve.wait_ge(bn1_done, t + 1)
                    dve.bn_aggr(mean_var1[:, t, :], stats1[:, t, :]).then_inc(ln1_stats, 1)
                dve.wait_ge(ln1_stats, tiles[-1] + 1)
                a, z = tiles[0], tiles[-1] + 1
                dve.tensor_scalar(var_eps1[:, a:z], mean_var1[:, a:z, 1], LN_EPS, None, ALU.add).then_inc(ln1_eps, 1)

            def modulate_gates(n, size, sign):
                g = mod_rows[:, n * B:(n + 1) * B, :]
                dve.tensor_scalar(size, g, -1.0, GATE_LEAST, ALU.mult, ALU.max).then_inc(gate_step, 1)
                dve.tensor_scalar(sign, g, 0.0, 2.0, ALU.is_ge, ALU.mult).then_inc(gate_step, 1)
                dve.wait_ge(gate_step, 3 * n + 2)
                dve.tensor_tensor(size, size, g, ALU.max).then_inc(gate_step, 1)
                dve.wait_ge(gate_step, 3 * n + 3)
                dve.scalar_tensor_tensor(out=g, in0=sign, scalar=1.0, in1=size,
                                         op0=ALU.subtract, op1=ALU.mult).then_inc(modr_done, 1)

            def reciprocal_roots(b):
                dve.tensor_scalar(norms[:, :, 0:HG], norms[:, :, 0:HG], 1.0 / D, RMS_EPS,
                                  ALU.mult, ALU.add).then_inc(newton_step, 1)
                dve.tensor_scalar(norms[:, :, HG:ALLH], norms[:, :, HG:ALLH], L2_EPS_SQUARED, None,
                                  ALU.max).then_inc(newton_step, 1)
                z, y, t = (norms[:, :, :].rearrange("p t h -> p (t h)"), rnorm[:, :, :].rearrange("p t h -> p (t h)"),
                           newton[:, :])
                at = b * 13 + 2
                dve.wait_ge(newton_step, at)
                dve.tensor_scalar(t.bitcast(I32), z.bitcast(I32), 1, None, ALU.logical_shift_right).then_inc(newton_step, 1)
                dve.wait_ge(newton_step, at + 1)
                dve.tensor_scalar(y.bitcast(I32), t.bitcast(I32), -1.0, float(0x5f3759df), ALU.mult,
                                  ALU.add).then_inc(newton_step, 1)
                for step in range(3):
                    dve.wait_ge(newton_step, at + 3 * step + 2)
                    dve.tensor_tensor(t, y, y, ALU.mult).then_inc(newton_step, 1)
                    dve.wait_ge(newton_step, at + 3 * step + 3)
                    dve.scalar_tensor_tensor(out=t, in0=t, scalar=-0.5, in1=z, op0=ALU.mult, op1=ALU.mult).then_inc(newton_step, 1)
                    dve.wait_ge(newton_step, at + 3 * step + 4)
                    dve.scalar_tensor_tensor(out=y, in0=t, scalar=1.5, in1=y, op0=ALU.add, op1=ALU.mult).then_inc(newton_step, 1)
                dve.wait_ge(newton_step, at + 11)

            def normalise_x(n):
                dve.wait_ge(hT_done, n * KC + 1)
                dve.tensor_copy(mods[:, :, :], mod_cols[:, :, :, bass.ds(n, 1)].rearrange(
                    "p n k o -> p n (k o)")).then_inc(mods_done, 1)
                for tt in range(TT):
                    dve.tensor_scalar(xhat[:, tt, :], x_tile(n, tt),
                                      mean_var1[:, bass.ds(n * TT + tt, 1), 0:1].rearrange("p a b -> p (a b)"),
                                      rstd1[:, bass.ds(n * TT + tt, 1)], ALU.subtract, ALU.mult).then_inc(xhat_done, 1)

            def square_sums(n):
                for tt in range(TT):
                    dve.wait_ge(qkv_sb, n * TT + tt + 1)
                    dve.tensor_tensor(squares[:, :], qkv[:, tt, :], qkv[:, tt, :], ALU.mult).then_inc(squared, 1)
                    dve.wait_ge(squared, n * TT + tt + 1)
                    dve.tensor_reduce(norms[:, tt, :], squares[:, :].rearrange("p (h d) -> p h d", d=D), AX.X,
                                      ALU.add).then_inc(sq_sum, 1)
                    dve.wait_ge(sq_sum, n * TT + tt + 1)

            def split_heads(n, parity, tt):
                m = n * TT + tt
                rn = rnorm[:, tt, :].rearrange("p (h o) -> p h o", o=1)
                v = qkv[:, tt, HG * D:].rearrange("p (h d) -> p h d", d=D)
                qk = qkv[:, tt, 0:HG * D].rearrange("p (h d) -> p h d", d=D)
                q, k = q6[:, tt % 2, :, :, :], k6[:, tt, :, :, :]
                dve.wait_ge(q_turned, 2 * m + 2)
                dve.wait_ge(k_turned, 2 * n + tt // 2 + 1)
                dve.tensor_tensor(qk, qk, rn[:, 0:HG, :].broadcast_to([P, HG, D]), ALU.mult).then_inc(rest_done, 1)
                dve.tensor_tensor(vn[:, parity, tt, :, :], v, rn[:, HG:, :].broadcast_to([P, G, D]),
                                  ALU.mult).then_inc(v_done, 1)
                dve.tensor_copy(v_aug[:, parity, tt, :, 0:D], v).then_inc(v_done, 1)
                dve.wait_ge(rest_done, 3 * m + 1)
                dve.tensor_copy(q[:, :, 0, :], qk[:, 0:H, :]).then_inc(hi_done, 1)
                dve.tensor_copy(k[:, :, 0, :], qk[:, H:, :]).then_inc(hi_done, 1)
                dve.wait_ge(hi_done, 2 * m + 2)
                dve.tensor_tensor(qk[:, 0:H, :], qk[:, 0:H, :], q[:, :, 0, :], ALU.subtract).then_inc(rest_done, 1)
                dve.tensor_tensor(qk[:, H:, :], qk[:, H:, :], k[:, :, 0, :], ALU.subtract).then_inc(rest_done, 1)
                dve.wait_ge(rest_done, 3 * m + 3)
                dve.tensor_copy(q[:, :, 1, :], qk[:, 0:H, :]).then_inc(mid_done, 1)
                dve.tensor_copy(k[:, :, 1, :], qk[:, H:, :]).then_inc(mid_done, 1)
                dve.wait_ge(mid_done, 2 * m + 2)
                dve.tensor_tensor(q[:, :, 5, :], qk[:, 0:H, :], q[:, :, 1, :], ALU.subtract).then_inc(lo_done, 1)
                dve.tensor_tensor(k[:, :, 4, :], qk[:, H:, :], k[:, :, 1, :], ALU.subtract).then_inc(lo_done, 1)

            def take_q(n, parity, tt):
                dve.wait_ge(q_turned, 2 * (n * TT + tt) + 1 + 4)
                dve.tensor_copy(qT[:, parity, 0:8, tt * P:(tt + 1) * P],
                                psM_b[0:QW, 0, :].rearrange("p (h t) -> p h t", h=8)).then_inc(trq_done, 1)

            def take_k(n, parity, pair):
                dve.wait_ge(k_turned, 2 * n + pair + 1 + 2)
                dve.tensor_copy(kT[:, parity, :, 2 * pair * P:2 * (pair + 1) * P],
                                psM_b[0:QW, 0, :].rearrange("p (h t) -> p h t", h=G)).then_inc(trk_done, 1)

            def take_sums(b, g):
                dve.wait_ge(pv_done, b * TT * G + (g + 1) * TT + 4)
                dve.tensor_copy(yT[:, g % 2, :], psY[:, g % 2, :]).then_inc(y_sb, 1)

            def finish_y(b, parity, g):
                m = b * G + g
                dve.wait_ge(yback_ps, m + 1)
                back = psM[:, g % 2, :].rearrange("p (t r w) -> p t r w", t=TT, r=R)
                dve.reciprocal(rden[:, :, :], back[:, :, :, D]).then_inc(rden_done, 1)
                dve.wait_ge(rden_done, m + 1)
                dve.tensor_tensor(yn[:, :, :, :], back[:, :, :, 0:D],
                                  rden[:, :, :].rearrange("p t (r o) -> p t r o", o=1).broadcast_to([P, TT, R, D]),
                                  ALU.mult).then_inc(yn_done, 1)
                dve.wait_ge(yn_done, m + 1 + G)
                vb = vn[:, parity, :, g:g + 1, :].broadcast_to([P, TT, R, D])
                dve.tensor_tensor(prod[:, :, :, :], yn[:, :, :, :], vb, ALU.mult).then_inc(prod_done, 1)
                dve.wait_ge(prod_done, m + 1)
                dve.tensor_reduce(dots[:, :, :], prod[:, :, :, :], AX.X, ALU.add).then_inc(dots_done, 1)
                dve.wait_ge(dots_done, m + 1)
                dve.tensor_tensor(prod[:, :, :, :], vb,
                                  dots[:, :, :].rearrange("p t (r o) -> p t r o", o=1).broadcast_to([P, TT, R, D]),
                                  ALU.mult).then_inc(along_done, 1)
                dve.wait_ge(along_done, m + 1)
                if g == 0:
                    dve.wait_ge(yT2_ps, (b + 1) * KC)
                dve.tensor_tensor(y_nat[:, :, g * R * D:(g + 1) * R * D].rearrange("p t (r d) -> p t r d", d=D),
                                  yn[:, :, :, :], prod[:, :, :, :], ALU.subtract).then_inc(y_done, 1)

            def add_attention(p):
                ga = mod_rows[:, bass.ds(p, 1), :].rearrange("p o c -> p (o c)")
                dve.wait_ge(h_out, 16 * p + 16)
                for tt in range(TT):
                    dve.wait_ge(o_ps, 2 * p + tt // 2 + 1)
                    dve.tensor_tensor(h_nat[:, tt, :], psM[:, tt // 2, (tt % 2) * C:(tt % 2 + 1) * C], ga,
                                      ALU.mult).then_inc(o_gated, 1)
                for tt in range(TT):
                    dve.wait_ge(o_gated, p * TT + tt + 1)
                    dve.tensor_tensor(x_tile(p, tt), x_tile(p, tt), h_nat[:, tt, :], ALU.add).then_inc(x2_done, 1)
                dve.wait_ge(x2_done, (p + 1) * TT)
                settle_v(dve, 2 * p)
                for tt in range(TT):
                    dve.bn_stats(stats[:, tt, :], x_tile(p, tt)).then_inc(bn_done, 1)
                dve.wait_ge(bn_done, (p + 1) * TT)
                settle_v(dve, 2 * p + 1)
                for tt in range(TT):
                    dve.bn_aggr(mean_var[:, tt, :], stats[:, tt, :]).then_inc(ln_stats, 1)
                dve.wait_ge(ln_stats, (p + 1) * TT)
                dve.tensor_scalar(var_eps[:, :], mean_var[:, :, 1], LN_EPS, None, ALU.add).then_inc(ln_eps, 1)

            def normalise_h(p, begin):
                dve.wait_ge(ln_rstd, p + 1)
                if begin:
                    dve.wait_ge(xT_ps, (p + 3) * KC)
                for tt in range(TT):
                    dve.tensor_scalar(xhat[:, tt, :], x_tile(p, tt), mean_var[:, tt, 0:1], rstd[:, tt:tt + 1],
                                      ALU.subtract, ALU.mult).then_inc(xhat2_done, 1)

            def experts_input(p):
                scale_row, shift_row = (mod_rows[:, bass.ds(at + p, 1), :].rearrange("p o c -> p (o c)")
                                        for at in (SCALE_ROW, SHIFT_ROW))
                for tt in range(TT):
                    dve.wait_ge(xhat2_done, p * TT + tt + 1)
                    dve.tensor_tensor(xhat[:, tt, :], xhat[:, tt, :], scale_row, ALU.mult).then_inc(h_scaled, 1)
                for tt in range(TT):
                    dve.wait_ge(h_scaled, p * TT + tt + 1)
                    dve.tensor_tensor(h_nat[:, tt, :], xhat[:, tt, :], shift_row, ALU.add).then_inc(h_done, 1)

            def take_logits(p):
                dve.wait_ge(logit_ps, p + 1 + 3)
                dve.tensor_copy(logits[:, bass.ds(p * TT, TT), :],
                                psM[:, 1, 0:TT * E].rearrange("p (t e) -> p t e", e=E)).then_inc(logit_done, 1)

            dve.wait_ge(x0_in, 16)
            mean_and_variance(range(TT))
            dve.wait_ge(modc_ps, 1)
            for n in range(2):
                dve.tensor_scalar(mod_cols[:, n, :, :], psM[:, 0, n * KC * B:(n + 1) * KC * B].rearrange(
                    "p (k b) -> p k b", b=B), float(n % 2), None, ALU.add).then_inc(modc_done, 1)
            dve.wait_ge(modc_done, 2)
            dve.wait_ge(ln1_rstd, 1)
            normalise_x(0)
            square_sums(0)
            reciprocal_roots(0)
            split_heads(0, 0, 0)
            split_heads(0, 0, 1)
            take_q(0, 0, 0)
            split_heads(0, 0, 2)
            take_q(0, 0, 1)
            split_heads(0, 0, 3)
            take_k(0, 0, 0)
            dve.wait_ge(x_in, 16 * (B - 1))
            mean_and_variance(range(TT, NT))
            take_q(0, 0, 2)
            take_q(0, 0, 3)
            take_k(0, 0, 1)
            dve.wait_ge(ln1_rstd, 2)

            def body(b, parity, begin, end):
                if begin:
                    normalise_x(b + 1)
                if end:
                    take_sums(b - 1, G - 1)
                    finish_y(b - 1, 1 - parity, G - 1)
                if begin:
                    square_sums(b + 1)
                take_sums(b, 0)
                if begin:
                    reciprocal_roots(b + 1)
                    split_heads(b + 1, 1 - parity, 0)
                finish_y(b, parity, 0)
                if begin:
                    split_heads(b + 1, 1 - parity, 1)
                if end:
                    add_attention(b - 1)
                if begin:
                    take_q(b + 1, 1 - parity, 0)
                    split_heads(b + 1, 1 - parity, 2)
                    take_q(b + 1, 1 - parity, 1)
                take_sums(b, 1)
                if begin:
                    take_k(b + 1, 1 - parity, 0)
                    split_heads(b + 1, 1 - parity, 3)
                else:
                    split_weights(0, 0)
                if end:
                    normalise_h(b - 1, begin)
                finish_y(b, parity, 1)
                if begin:
                    take_q(b + 1, 1 - parity, 2)
                if end:
                    experts_input(b - 1)
                if begin:
                    take_q(b + 1, 1 - parity, 3)
                take_sums(b, 2)
                if begin:
                    take_k(b + 1, 1 - parity, 1)
                finish_y(b, parity, 2)
                if end:
                    take_logits(b - 1)
                else:
                    dve.wait_ge(mod_in, 64)
                    dve.wait_ge(xT_ps, 2 * KC)
                    modulate_gates(0, xhat[:, :, :], h_nat[:, :, :])
                    dve.tensor_scalar(mod_rows[:, SCALE_ROW:, :], mod_rows[:, SCALE_ROW:, :], 1.0, None,
                                      ALU.add).then_inc(modr_done, 1)
                    dve.wait_ge(modr_done, 2)

            def choose_experts(n):
                a, z = ((0, NT - TT), (NT - TT, NT))[n]
                at, tiles = ROUTE_STEPS * n, z - a
                logit, p, top, total = logits[:, a:z, :], rt_p[:, a:z, :], rt_max[:, a:z], rt_sum[:, a:z]
                ge, gt = (probs[:, buf, :, :].rearrange("p r n -> p (r n)")[:, a * E * E:z * E * E].rearrange(
                    "p (t e j) -> p t e j", e=E, j=E) for buf in range(2))
                ahead = rt_before[:, a:z, :]
                dve.wait_ge(logit_done, (B - 1, B)[n] + 2)
                dve.tensor_reduce(top, logit, AX.X, ALU.max).then_inc(rt_step, 1)
                dve.wait_ge(rt_step, at + 1)
                wide = lambda v: v.rearrange("p (t o) -> p t o", o=1).broadcast_to([P, tiles, E])
                dve.tensor_tensor(p, logit, wide(top), ALU.subtract).then_inc(rt_step, 1)
                dve.wait_ge(rt_exp, n + 1)
                dve.tensor_reduce(total, p, AX.X, ALU.add).then_inc(rt_step, 1)
                dve.wait_ge(rt_step, at + 3)
                dve.reciprocal(total, total).then_inc(rt_step, 1)
                dve.wait_ge(rt_step, at + 4)
                dve.tensor_tensor(p, p, wide(total), ALU.mult).then_inc(rt_step, 1)
                dve.wait_ge(rt_step, at + 5)
                other = p.rearrange("p t (o e) -> p t o e", o=1).broadcast_to([P, tiles, E, E])
                own = p.rearrange("p t (e o) -> p t e o", o=1).broadcast_to([P, tiles, E, E])
                ties = tie[:, :, :].rearrange("p (o e) j -> p o e j", o=1).broadcast_to([P, tiles, E, E])
                dve.tensor_tensor(ge, other, own, ALU.is_ge).then_inc(rt_step, 1)
                dve.tensor_tensor(gt, other, own, ALU.is_gt).then_inc(rt_step, 1)
                dve.wait_ge(rt_step, at + 7)
                dve.tensor_tensor(ge, ge, ties, ALU.mult).then_inc(rt_step, 1)
                dve.wait_ge(rt_step, at + 8)
                dve.tensor_tensor(gt, gt, ge, ALU.max).then_inc(rt_step, 1)
                dve.wait_ge(rt_step, at + 9)
                dve.tensor_tensor(gt, gt, other, ALU.mult).then_inc(rt_step, 1)
                dve.wait_ge(rt_step, at + 10)
                dve.tensor_reduce(ahead, gt, AX.X, ALU.add).then_inc(rt_step, 1)
                dve.wait_ge(rt_step, at + 11)
                dve.tensor_scalar(keep[:, a:z, :], ahead, TOP_P, None, ALU.is_le).then_inc(rt_step, 1)
                dve.wait_ge(rt_step, at + 12)
                dve.tensor_tensor(moe_w[:, a:z, :], keep[:, a:z, :], p, ALU.mult).then_inc(rt_kept, 1)
                dve.tensor_copy(keep_b[:, a:z, :], keep[:, a:z, :]).then_inc(rt_kept, 1)

            dve.wait_ge(consts, NCONST)
            attention(dve, body)
            take_sums(B - 1, G - 1)
            finish_y(B - 1, (B - 1) % 2, G - 1)
            choose_experts(0)
            add_attention(B - 1)
            normalise_h(B - 1, False)
            experts_input(B - 1)
            take_logits(B - 1)

            choose_experts(1)

            at = [2 * ROUTE_STEPS]

            def step(ins):
                at[0] += 1
                ins.then_inc(rt_step, 1)
                dve.wait_ge(rt_step, at[0])

            dve.wait_ge(rank_ps, 1)
            tiles = psM[:, 1, 0:NT * E].rearrange("p (t e) -> p t e", e=E)
            step(dve.tensor_copy(run[0][:, :, :], tiles))
            hop = 1
            while hop < NT:
                old, new = run
                dve.tensor_copy(new[:, 0:hop, :], old[:, 0:hop, :]).then_inc(rt_step, 1)
                at[0] += 1
                step(dve.tensor_tensor(new[:, hop:, :], old[:, hop:, :], old[:, 0:NT - hop, :], ALU.add))
                run.reverse()
                hop *= 2
            total = run[0]
            step(dve.tensor_copy(rank[:, :, :], psM[:, 0, 0:NT * E].rearrange("p (t e) -> p t e", e=E)))
            step(dve.tensor_tensor(rank[:, 1:, :], rank[:, 1:, :], total[:, 0:NT - 1, :], ALU.add))
            step(dve.tensor_copy(rank_i[:, :, :], rank[:, :, :]))
            step(dve.tensor_scalar(tile_i[:, :, :], rank_i[:, :, :], 7, None, ALU.logical_shift_right))
            step(dve.tensor_scalar(row_i[:, :, :], rank_i[:, :, :], P - 1, None, ALU.bitwise_and))
            step(dve.tensor_copy(tile_h[:, :, :], tile_i[:, :, :]))
            step(dve.tensor_copy(row_f[:, :, :], row_i[:, :, :]))
            step(dve.scalar_tensor_tensor(out=row_f[:, :, :], in0=row_f[:, :, :], scalar=1.0, in1=keep[:, :, :],
                                          op0=ALU.add, op1=ALU.mult))
            step(dve.tensor_scalar(row_h[:, :, :], row_f[:, :, :].rearrange("p t e -> p e t"), -1.0, None, ALU.add))
            dve.wait_ge(h_out, 16 * (B + 1))
            by_tile = one_tile[:, :, :, :].rearrange("p s t e -> p s (t e)")

            def every_slot(v):
                return v.rearrange("p (o t) e -> p o (t e)", o=1).broadcast_to([P, TSLOTS, NT * E])

            step(dve.tensor_tensor(by_tile, slot_tile[:, :, :, :].rearrange("p s t e -> p s (t e)"),
                                   every_slot(tile_h[:, :, :]), ALU.is_equal))
            step(dve.tensor_tensor(by_tile, by_tile, every_slot(token1[:, :, :]), ALU.mult))
            for e in range(E):
                if e >= 2:
                    dve.wait_ge(lists_ps, e - 1)
                dve.tensor_tensor(one_row[:, e % 2, :, :], slot_row[:, :, :],
                                  row_h[:, e:e + 1, :].broadcast_to([P, P, NT]), ALU.is_equal).then_inc(one_done, 1)
            step(dve.tensor_copy(cnt_i[:, :], total[:, NT - 1, :]))
            step(dve.tensor_scalar(items_f[:, :], cnt_i[:, :], float(SW - 1), None, ALU.add))
            step(dve.tensor_copy(cnt_i[:, :], items_f[:, :]))
            step(dve.tensor_scalar(meta[:, 0, :], cnt_i[:, :], 8, None, ALU.logical_shift_right))
            step(dve.tensor_scalar(meta[:, 0, :], meta[:, 0, :], 1.0, None, ALU.max))
            step(dve.tensor_copy(items_f[:, :], meta[:, 0, :]))
            step(dve.tensor_copy(cnt_f[0][:, :], items_f[:, :]))
            hop = 1
            while hop < E:
                old, new = cnt_f
                dve.tensor_copy(new[:, 0:hop], old[:, 0:hop]).then_inc(rt_step, 1)
                at[0] += 1
                step(dve.tensor_tensor(new[:, hop:], old[:, hop:], old[:, 0:E - hop], ALU.add))
                cnt_f.reverse()
                hop *= 2
            step(dve.tensor_copy(meta[:, 2, :], cnt_f[0][:, :]))
            step(dve.tensor_tensor(items_f[:, :], cnt_f[0][:, :], items_f[:, :], ALU.subtract))
            dve.tensor_copy(meta[:, 1, :], items_f[:, :]).then_inc(meta_ready, 1)
            dve.wait_ge(lists_ps, E)
            lists = psY[:, 0, 0:E * TSLOTS].rearrange("p (e s) -> p e s", e=E)
            pads = pad_row[:, :, :, :].rearrange("p e s k -> p e (s k)")
            step(dve.scalar_tensor_tensor(out=is_pad[:, :, :], in0=lists, scalar=0.0, in1=pads, op0=ALU.is_equal,
                                          op1=ALU.mult))
            dve.scalar_tensor_tensor(out=ids_i[:, :, :], in0=lists, scalar=-1.0, in1=is_pad[:, :, :], op0=ALU.add,
                                     op1=ALU.add).then_inc(rt_step, 1)
            dve.tensor_scalar(idx_all[:, :].rearrange("p (s k) -> p s k", k=2),
                              pad_row[:, 0, 0:1, :].broadcast_to([P, S * ITEMS // 2 + TSLOTS, 2]), -1.0, None,
                              ALU.add).then_inc(idx_ready, 1)
            dve.wait_ge(rt_step, at[0] + 1)
            dve.wait_ge(meta_ready, 1)
            for e in range(E):
                before = dve.value_load(meta[0:1, 1, e:e + 1], min_val=0, max_val=ITEMS)
                dve.wait_ge(idx_ready, e + 1)
                dve.tensor_copy(idx_all[:, bass.ds(S * before, TSLOTS)], ids_i[:, e, :]).then_inc(idx_ready, 1)

            def split_input(m):
                dve.wait_ge(sel_hi, m + 1)
                dve.tensor_tensor(hs_lo[:, :, :].rearrange("p k t -> p (k t)"), psM[:, 0, :],
                                  hs_hi[:, :, :].rearrange("p k t -> p (k t)").bitcast(F32), ALU.subtract).then_inc(sel_lo, 1)

            def product(m, h):
                dve.wait_ge(silu_ready, 2 * m + h + 1 + FREE)
                dve.wait_ge(up_ps, 2 * m + h + 1)
                dve.tensor_tensor(a_full[:, h, :], psS[:, 1, h, :], silu_g[:, h, :], ALU.mult).then_inc(a_ready, 1)

            def split_hidden(m, h):
                dve.wait_ge(a_ready, 2 * m + h + 1 + FREE)
                dve.wait_ge(a_rounded, 2 * m + h + 1)
                dve.tensor_tensor(a_lo[:, 2 * h:2 * h + 2, :].rearrange("p i t -> p (i t)"), a_full[:, h, :],
                                  a_hi[:, 2 * h:2 * h + 2, :].rearrange("p i t -> p (i t)").bitcast(F32),
                                  ALU.subtract).then_inc(a_split, 1)

            def output(e1, m):
                dve.wait_ge(down_ps, 2 * m + 2 + FREE)
                dve.wait_ge(scattered, ZEROING + 32 * m)
                dve.wait_ge(w_copied, m + 1)
                for k in range(S):
                    dve.tensor_scalar(y_sel[:, k, :], psY[:, k, 0:C],
                                      w_sel[:, bass.ds(m + 1, 1), k, bass.ds(e1, 1)].rearrange("p a b -> p (a b)"), None,
                                      ALU.mult).then_inc(y_ready, 1)

            def body(e, e2, first, m, half):
                product(m, 0)
                split_input(m + 1)
                split_hidden(m, 0)
                product(m, 1)
                if first and half == 0:
                    with dve.If(e2 > 0):
                        output(e, m - 1)
                else:
                    output(e if first else e + 1, m - 1)
                split_hidden(m, 1)

            def between_experts(e, e2, half, before):
                if half == 0:
                    split_weights(e + 1, 1)
                else:
                    with dve.If(e2 < E // 2 - 1):
                        split_weights(e + 1, 0)

            split_input(0)
            walk_items(dve, body, between_experts)
            items = dve.value_load(meta[0:1, 2, E - 1:E], min_val=E, max_val=ITEMS)
            output(E, items - 1)
            modulate_gates(1, y_all[:, 0:B, :], y_all[:, B:2 * B, :])
            dve.wait_ge(modr_done, 3)
            for b in range(B):
                y, tiles = y_all[:, b * TT:(b + 1) * TT, :], slice(b * TT, (b + 1) * TT)
                dve.wait_ge(y_in[b], 16)
                dve.tensor_tensor(y, y, mod_rows[:, B + b:B + b + 1, :].broadcast_to([P, TT, C]), ALU.mult).then_inc(out_step, 1)
                dve.wait_ge(out_step, b + 1)
                dve.tensor_tensor(y, y, x_all[:, tiles, :], ALU.add).then_inc(out_ready, 1)

        @block.tensor
        def _(pe):
            for freed, n in ((q_turned, 4), (k_turned, 2), (pv_done, 4), (yT2_ps, KC), (logit_ps, 3), (down_ps, FREE)):
                pe.sem_inc(freed, n)
            pe.wait_ge(wmod_in, 16)
            pe.wait_ge(silu_step, 4)
            for n, m in enumerate((SHIFT_A, SCALE_A)):
                for k in range(KC):
                    for j in range(KC):
                        mm = pe.matmul(psM[:, 0, (n * KC + k) * B:(n * KC + k + 1) * B],
                                       w_mod[:, j, m * C + k * P:m * C + (k + 1) * P], silu_c[:, j, :],
                                       start=j == 0, stop=j == KC - 1)
            mm.then_inc(modc_ps, 1)
            def turn_x(n, first):
                pe.wait_ge(xhat_done, (n + 1) * TT)
                if not first:
                    pe.wait_ge(hT2_done, n * KC)
                    pe.wait_ge(yn_done, (n - 1) * G + G - 1)
                    pe.wait_ge(trk_done, 2 * n)
                    pe.wait_ge(tr_done, n * TT)
                    pe.wait_ge(logit_done, n)
                for k in range(KC):
                    for tt in range(TT):
                        mm = pe.transpose(psM[:, k, tt * P:(tt + 1) * P], xhat[:, tt, k * P:(k + 1) * P], ident[:, :])
                    mm.then_inc(xT_ps, 1)

            def project_qkv(n, first, pair):
                if pair == 0:
                    pe.wait_ge(hT_done, (n + 1) * KC + 1)
                    if not first:
                        pe.wait_ge(yn_done, n * G)
                else:
                    pe.wait_ge(qkv_sb, n * TT + 2)
                for tt in (2 * pair, 2 * pair + 1):
                    for k in range(KC):
                        mm = pe.matmul(psM[:, tt % 2, 0:QKV], hT[:, k, tt * P:(tt + 1) * P], w_qkv[:, k, :],
                                       start=k == 0, stop=k == KC - 1)
                    mm.then_inc(qkv_ps, 1)

            def turn_q(n, first, end, tt):
                m = n * TT + tt
                pe.wait_ge(parts_done, 4 * (m + 1))
                pe.wait_ge(lo_done, 2 * (m + 1) + 1)
                if tt == 0:
                    pe.wait_ge(qkv_sb, (n + 1) * TT)
                    if end:
                        pe.wait_ge(o_gated, (n - 1) * TT)
                    elif not first:
                        pe.wait_ge(yn_done, (n - 1) * G + 1 + G)
                elif tt == 2:
                    pe.wait_ge(trk_done, 2 * n + 1)
                    pe.wait_ge(tr_done, n * TT + tt)
                    if not first:
                        pe.wait_ge(yn_done, (n - 1) * G + 2 + G)
                else:
                    pe.wait_ge(trq_done, n * TT + tt)
                    pe.wait_ge(tr_done, n * TT + tt)
                for half in range(2):
                    for j in range(H // 2):
                        mm = pe.transpose(psM_b[0:QW, half, j * P:(j + 1) * P],
                                          q6[:, tt % 2, half * H // 2 + j, :, :].rearrange("p a d -> p (a d)"), ident_b[:, :])
                    mm.then_inc(q_turned, 1)

            def turn_k(n, pair):
                pe.wait_ge(trq_done, n * TT + 2 * pair + 2)
                for tt in (2 * pair, 2 * pair + 1):
                    for j in range(G):
                        at = (2 * j + tt % 2) * P
                        mm = pe.transpose(psM_b[0:QW, 0, at:at + P], k6[:, tt, j, :, :].rearrange("p a d -> p (a d)"),
                                          ident_b[:, :])
                mm.then_inc(k_turned, 1)

            def score(b, parity, u):
                gk, pair = u // 2, u % 2
                g, kt = gk // TT, gk % TT
                if u < 2:
                    pe.wait_ge(trq_done, (b + 1) * TT)
                    pe.wait_ge(tr_done, (b + 1) * TT)
                    pe.wait_ge(trk_done, 2 * (b + 1))
                pe.wait_ge(probs_done, b * UNITS + u + 1)
                for j in range(2):
                    mm = pe.matmul(psS[:, u % 2, j, :], kT[:, parity, g, kt * P:(kt + 1) * P],
                                   qT[:, parity, g * R + 2 * pair + j, :], start=True, stop=True)
                mm.then_inc(scores, 1)

            def turn_y(b, g, begin, end):
                pe.wait_ge(y_sb, b * G + g + 1 + 2)
                if g == 0:
                    if begin:
                        pe.wait_ge(qkv_sb, (b + 2) * TT)
                    if end:
                        pe.wait_ge(yT2_done, b * KC)
                elif g == G - 1:
                    pe.wait_ge(logit_done, b + 2)
                    if begin:
                        pe.wait_ge(hT_done, (b + 3) * KC + 1)
                else:
                    if begin and g == 1:
                        pe.wait_ge(tr_done, (b + 1) * TT + 2)
                    if begin and g == 2:
                        pe.wait_ge(trk_done, 2 * (b + 1) + 2)
                    if end:
                        pe.wait_ge(o_gated, b * TT)
                for tt in range(TT):
                    mm = pe.transpose(psM[:, g % 2, tt * P:(tt + 1) * P], yT[:, g % 2, tt * P:(tt + 1) * P],
                                      ident[:, :])
                mm.then_inc(yback_ps, 1)

            def turn_outputs(p, begin):
                pe.wait_ge(y_done, (p + 1) * G)
                pe.wait_ge(hT2_done, (p + 2) * KC)
                if begin:
                    pe.wait_ge(qkv_sb, (p + 3) * TT)
                for k in range(KC):
                    for tt in range(TT):
                        mm = pe.transpose(psM[:, k, tt * P:(tt + 1) * P], y_nat[:, tt, k * P:(k + 1) * P], ident[:, :])
                    mm.then_inc(yT2_ps, 1)

            def project_outputs(p, within):
                pe.wait_ge(yT2_done, (p + 1) * KC)
                if within:
                    pe.wait_ge(yn_done, (p + 1) * G + 1 + G)
                for tt in range(TT):
                    for k in range(KC):
                        mm = pe.matmul(psM[:, tt // 2, (tt % 2) * C:(tt % 2 + 1) * C], hT[:, k, tt * P:(tt + 1) * P],
                                       w_o[:, k, :], start=k == 0, stop=k == KC - 1)
                    if tt % 2:
                        mm.then_inc(o_ps, 1)

            def turn_h(p, nth, begin, within):
                k = KC - 1 - nth
                pe.wait_ge(h_done, (p + 1) * TT)
                if nth == 0 and begin:
                    pe.wait_ge(tr_done, (p + 3) * TT)
                elif within:
                    pe.wait_ge(yn_done, (p + 1) * G + 2 + nth + G)
                for tt in range(TT):
                    mm = pe.transpose(psM[:, k, tt * P:(tt + 1) * P], h_nat[:, tt, k * P:(k + 1) * P], ident[:, :])
                mm.then_inc(h_turned, 1)

            def route(p):
                pe.wait_ge(hT2_done, (p + 3) * KC)
                for tt in range(TT):
                    for k in range(KC):
                        mm = pe.matmul(psM[:, 1, tt * E:(tt + 1) * E], hT[:, k, tt * P:(tt + 1) * P], w_r[:, k, :],
                                       start=k == 0, stop=k == KC - 1)
                mm.then_inc(logit_ps, 1)

            pe.wait_ge(ident_done, 2)
            pe.wait_ge(modc_done, 2)
            turn_x(0, True)
            pe.wait_ge(wattn_in, 48)
            project_qkv(0, True, 0)
            project_qkv(0, True, 1)
            pe.wait_ge(wmod_rest_in, 16)
            for n in range(2):
                at = (GATE_A + 2 * n) * C
                for j in range(KC):
                    mm = pe.matmul(psY[0:B, n, 0:2 * C], silu_c[:, j, :], w_mod[:, j, at:at + 2 * C],
                                   start=j == 0, stop=j == KC - 1)
                mm.then_inc(modr_ps, 1)
            for pair in range(2):
                turn_q(0, True, False, 2 * pair)
                turn_q(0, True, False, 2 * pair + 1)
                turn_k(0, pair)
            pe.wait_ge(wrest_in, 32)
            pe.wait_ge(consts, NCONST)
            score(0, 0, 0)
            score(0, 0, 1)
            pe.wait_ge(row_copied, 2)

            def body(b, parity, begin, end):
                pe.wait_ge(v_done, 2 * (b + 1) * TT + 1)
                for gk in range(G * TT):
                    g, kt = gk // TT, gk % TT
                    if gk + 1 < G * TT:
                        score(b, parity, 2 * gk + 2)
                        score(b, parity, 2 * gk + 3)
                    elif begin:
                        score(b + 1, 1 - parity, 0)
                        score(b + 1, 1 - parity, 1)
                    if kt == 0:
                        pe.wait_ge(y_sb, b * G + g + 1)
                    pe.wait_ge(probs_done, b * UNITS + 2 * gk + 2 + 2)
                    for r in range(R):
                        mm = pe.matmul(psY[r * YROWS:(r + 1) * YROWS, g % 2, :], v_aug[:, parity, kt, g, :],
                                       probs[:, gk % 4, r, :], start=kt == 0, stop=kt == TT - 1)
                    mm.then_inc(pv_done, 1)
                    if begin:
                        if gk == 0:
                            turn_x(b + 1, False)
                        elif gk in (2, 3):
                            project_qkv(b + 1, False, gk - 2)
                        elif gk in (7, 8, 10, 11):
                            turn_q(b + 1, False, end, {7: 0, 8: 1, 10: 2, 11: 3}[gk])
                        elif gk in (9, 12):
                            turn_k(b + 1, (gk - 9) // 3)
                    if gk in (5, 9, 13):
                        turn_y(b, (gk - 5) // 4, begin, end)
                    if end:
                        if gk == 1:
                            turn_y(b - 1, G - 1, begin, end)
                        elif gk == 4:
                            turn_outputs(b - 1, begin)
                        elif gk == 6:
                            project_outputs(b - 1, True)
                        elif gk in (12, 14):
                            turn_h(b - 1, (gk - 12) // 2, begin, True)
                        elif gk == 15:
                            route(b - 1)

            attention(pe, body)
            turn_y(B - 1, G - 1, False, True)
            turn_outputs(B - 1, False)
            project_outputs(B - 1, False)
            turn_h(B - 1, 0, False, False)
            turn_h(B - 1, 1, False, False)
            route(B - 1)

            pe.wait_ge(rt_kept, 4)
            kept = keep_b[:, :, :].rearrange("p t e -> p (t e)")
            pe.matmul(psM[:, 0, 0:NT * E], earlier[:, :], kept, start=True, stop=True)
            pe.matmul(psM[:, 1, 0:NT * E], ones_b[:, :], kept, start=True, stop=True).then_inc(rank_ps, 1)
            pe.wait_ge(y_sb, B * G + 2)
            pe.wait_ge(probs_done, B * UNITS + 2)
            for e in range(E):
                pe.wait_ge(one_done, e + 1)
                for tt in range(NT):
                    mm = pe.matmul(psY[:, 0, e * TSLOTS:(e + 1) * TSLOTS], one_row[:, e % 2, :, tt],
                                   one_tile[:, :, tt, e], start=tt == 0, stop=tt == NT - 1)
                mm.then_inc(lists_ps, 1)

            def turn(m):
                pe.wait_ge(gathered, 32 * (m + 1))
                for k in range(KC):
                    for j in range(S):
                        mm = pe.transpose(psM[:, 0, k * SW + j * P:k * SW + (j + 1) * P], h_sel[:, j, k * P:(k + 1) * P],
                                          ident[:, :])
                mm.then_inc(turned, 1)

            def gate_up(m, half, h):
                for part, (ps, ready, used) in enumerate(((psS[:, 0, h, :], gate_ps, silu_ready),
                                                          (psS[:, 1, h, :], up_ps, a_ready))):
                    pe.wait_ge(used, 2 * m + h - 1 + FREE)
                    for i in range(2):
                        at = 0
                        for k in range(KC):
                            cols = slice(k * I + (2 * h + i) * P, k * I + (2 * h + i + 1) * P)
                            hi, lo = w_hi[half][part][:, cols], w_lo[half][part][:, cols]
                            for w, v in ((hi, hs_hi), (hi, hs_lo), (lo, hs_hi)):
                                mm = pe.matmul(ps[:, i * SW:(i + 1) * SW], w, v[:, k, :], start=at == 0, stop=at == 3 * KC - 1)
                                at += 1
                    mm.then_inc(ready, 1)

            def down(m, half, h):
                pe.wait_ge(a_split, 2 * m + h + 1 + FREE)
                if h == 0:
                    pe.wait_ge(y_ready, 2 * m + FREE)
                for j in range(S):
                    tok = slice(j * P, (j + 1) * P)
                    for i in (2 * h, 2 * h + 1):
                        hi, lo = (w[half][2][:, i * C:(i + 1) * C] for w in (w_hi, w_lo))
                        for n, (v, w) in enumerate(((a_hi, hi), (a_hi, lo), (a_lo, hi))):
                            mm = pe.matmul(psY[:, j, 0:C], v[:, i, tok], w, start=i == 0 and n == 0, stop=i == KI - 1 and n == 2)
                mm.then_inc(down_ps, 1)

            def downs(m, half):
                down(m, half, 0)
                down(m, half, 1)

            def body(e, e2, first, m, half):
                if first:
                    pe.wait_ge(w_ready, 3 * e + 3)
                pe.wait_ge(sel_lo, m + 1)
                gate_up(m, half, 0)
                turn(m + 1)
                gate_up(m, half, 1)
                if first and half == 0:
                    with pe.If(e2 > 0):
                        downs(m - 1, 1)
                else:
                    downs(m - 1, 1 - half if first else half)

            pe.wait_ge(meta_ready, 1)
            turn(0)
            walk_items(pe, body, lambda *a: None)
            items = pe.value_load(meta[0:1, 2, E - 1:E], min_val=E, max_val=ITEMS)
            downs(items - 1, 1)


_INS = ["x", "wqT", "wkT", "wvT", "woT", "routerT", "gateT", "upT", "downT", "cT", "wmod"]


def kernel(L0_attn_x, L0_attn_Wq, L0_attn_Wk, L0_attn_Wv, L0_attn_Wo, L0_ffn_router_w, L0_ffn_gate_w, L0_ffn_up_w,
           L0_ffn_down_w, L0_c, L0_wmod):
    import concourse.bacc as bacc
    import numpy as np
    from concourse.bass_utils import run_bass_kernel_spmd

    turned = [np.swapaxes(w, -1, -2) for w in (L0_attn_Wq, L0_attn_Wk, L0_attn_Wv, L0_attn_Wo, L0_ffn_router_w,
                                               L0_ffn_gate_w, L0_ffn_up_w, L0_ffn_down_w, L0_c)]
    arrays = dict(zip(_INS, map(np.ascontiguousarray, [L0_attn_x, *turned, L0_wmod])))
    nc = bacc.Bacc("TRN2", target_bir_lowering=False, num_devices=1)
    args = [nc.dram_tensor(k, v.shape, mybir.dt.from_np(v.dtype), kind="ExternalInput").ap() for k, v in arrays.items()]
    out = nc.dram_tensor("out", arrays["x"].shape, mybir.dt.from_np(arrays["x"].dtype), kind="ExternalOutput").ap()
    adaln_block(nc, *args, out)
    return run_bass_kernel_spmd(nc, [arrays], core_ids=[0]).results[0]["out"]
```
